# Optimizing a Trainium2 kernel written in Bass

```python
import numpy as np
import jax
import jax.numpy as jnp

def _softmax(x, axis=-1):
    return jax.nn.softmax(x, axis=axis)

def _gelu(x):
    return jax.nn.gelu(x, approximate=True)

def _silu(x):
    return jax.nn.silu(x)

def _sigmoid(x):
    return jax.nn.sigmoid(x)

def _layernorm(x, axis=-1, eps=1e-05):
    m = jnp.mean(x, axis=axis, keepdims=True)
    v = jnp.var(x, axis=axis, keepdims=True)
    return (x - m) / jnp.sqrt(v + eps)

def _scatter_add(tgt, idx, src, axis=0):
    return tgt.at[idx].add(src)

def _segment_sum(src, seg, n):
    return jax.ops.segment_sum(src, seg, n)
kernel_name = 'mk_adj_ffn_d1_adj_r2_972fdc'

def setup_inputs(seed: int=0):
    np.random.seed(seed)
    _w = jnp.asarray

    def _rec_inputs():
        import jax
        import jax.numpy as jnp
        _gk = jax.random.key(seed)
        x = -0.0005207 + 1.001 * jax.random.normal(jax.random.fold_in(_gk, 1), (128, 128, 128), jnp.float32)
        _w = (1.0 + jnp.arange(128, dtype=jnp.float32)) ** (-0.5)
        _w = _w / _w.mean()
        _pij = jnp.clip(0.125 * _w[:, None] * _w[None, :], 0.0, 1.0)
        _a = jax.random.uniform(jax.random.fold_in(_gk, 2), (128, 128, 128)) < _pij
        adj = _a.astype(jnp.int32)
        return (x, adj)
    x, adj = _rec_inputs()

    def _L0_gnn_setup():
        import jax, jax.numpy as jnp
        import numpy as np
        B, N, F_IN, F_OUT = (1, 4096, 128, 128)
        ALPHA = 0.2
        NEG_INF = -9000000000000000.0
        key = jax.random.key(seed)
        ks = jax.random.split(key, 8)
        feat = jax.random.normal(ks[0], (B, N, F_IN), dtype=jnp.float32)
        adj = jax.random.randint(ks[1], (B, N, N), 0, 2, dtype=jnp.int32)
        s = 1.414 * (6.0 / (F_IN + F_OUT)) ** 0.5
        W = jax.random.uniform(ks[2], (F_IN, F_OUT), minval=-s, maxval=s, dtype=jnp.float32)
        a_1 = jax.random.normal(ks[3], (F_OUT, 1), dtype=jnp.float32) * 0.1
        a_2 = jax.random.normal(ks[4], (F_OUT, 1), dtype=jnp.float32) * 0.1
        a_12 = jax.random.normal(ks[5], (F_OUT, F_OUT), dtype=jnp.float32) * (1.0 / F_OUT ** 0.5)
        W_1 = jax.random.uniform(ks[6], (F_IN, F_OUT), minval=-s, maxval=s, dtype=jnp.float32)
        W_2 = jax.random.uniform(ks[7], (F_IN, F_OUT), minval=-s, maxval=s, dtype=jnp.float32)
        return {'feat': feat, 'adj': adj, 'W': W, 'a_1': a_1, 'a_2': a_2, 'a_12': a_12, 'W_1': W_1, 'W_2': W_2}
    _L0_gnn_all = _L0_gnn_setup()
    _L0_gnn_in = {k: v for k, v in _L0_gnn_all.items() if k in ('W', 'a_1', 'a_2', 'a_12', 'W_1', 'W_2')}
    del _L0_gnn_all

    def _L0_ffn_setup():
        import jax, jax.numpy as jnp
        import numpy as np
        C = 128
        HID = 512
        E = 8
        TEMP = 1.0
        key = jax.random.key(seed)
        ks = jax.random.split(key, 7)
        x = jax.random.normal(ks[0], (8, 8192, C), dtype=jnp.float32)
        W1 = jax.random.normal(ks[1], (C, HID), dtype=jnp.float32) * 0.02
        b1 = jnp.zeros((HID,), dtype=jnp.float32)
        Wg = jax.random.normal(ks[2], (HID, E), dtype=jnp.float32) * 0.02
        bg = jnp.zeros((E,), dtype=jnp.float32)
        Wd = jax.random.normal(ks[3], (E, HID, C), dtype=jnp.float32) * 0.02
        bd = jnp.zeros((E, C), dtype=jnp.float32)
        return {'x': x, 'W1': W1, 'b1': b1, 'Wg': Wg, 'bg': bg, 'Wd': Wd, 'bd': bd}
    _L0_ffn_all = _L0_ffn_setup()
    _L0_ffn_in = {k: v for k, v in _L0_ffn_all.items() if k in ('W1', 'b1', 'Wg', 'bg', 'Wd', 'bd')}
    del _L0_ffn_all
    return {'x': x, 'adj': adj, 'L0_gnn_W': _L0_gnn_in['W'], 'L0_gnn_a_1': _L0_gnn_in['a_1'], 'L0_gnn_a_2': _L0_gnn_in['a_2'], 'L0_gnn_a_12': _L0_gnn_in['a_12'], 'L0_gnn_W_1': _L0_gnn_in['W_1'], 'L0_gnn_W_2': _L0_gnn_in['W_2'], 'L0_ffn_W1': _L0_ffn_in['W1'], 'L0_ffn_b1': _L0_ffn_in['b1'], 'L0_ffn_Wg': _L0_ffn_in['Wg'], 'L0_ffn_bg': _L0_ffn_in['bg'], 'L0_ffn_Wd': _L0_ffn_in['Wd'], 'L0_ffn_bd': _L0_ffn_in['bd']}

def reference(x, adj, L0_gnn_W, L0_gnn_a_1, L0_gnn_a_2, L0_gnn_a_12, L0_gnn_W_1, L0_gnn_W_2, L0_ffn_W1, L0_ffn_b1, L0_ffn_Wg, L0_ffn_bg, L0_ffn_Wd, L0_ffn_bd):
    import jax
    import jax.numpy as jnp

    def _L0_gnn_ref(feat, adj, W, a_1, a_2, a_12, W_1, W_2):
        import jax, jax.numpy as jnp
        import numpy as np
        B, N, F_IN, F_OUT = (1, 4096, 128, 128)
        ALPHA = 0.2
        NEG_INF = -9000000000000000.0
        h = jnp.matmul(feat, W)
        Ax = jnp.matmul(h, a_1)
        Ay = jnp.matmul(h, a_2)
        A_xy = jnp.matmul(jnp.matmul(h, a_12), jnp.swapaxes(h, 1, 2))
        logits = jnp.swapaxes(Ax, 1, 2) + Ay + A_xy
        e = jax.nn.leaky_relu(logits, negative_slope=ALPHA)
        e = jnp.where(adj > 0, e, NEG_INF)
        attention = jax.nn.softmax(e, axis=-1)
        h_prime = jnp.matmul(attention, feat)
        h_out = jnp.matmul(feat, W_1) + jnp.matmul(h_prime, W_2)
        return jax.nn.elu(h_out)

    def _L0_ffn_ref(x, W1, b1, Wg, bg, Wd, bd):
        import jax, jax.numpy as jnp
        import numpy as np
        C = 128
        HID = 512
        E = 8
        TEMP = 1.0
        orig_shape = x.shape
        xf = x.reshape(-1, orig_shape[-1])
        H = jax.nn.gelu(xf @ W1 + b1, approximate=False)
        probs = jax.nn.softmax((H @ Wg + bg) / TEMP, axis=-1)
        assign = jnp.argmax(probs, axis=-1)
        out = jnp.zeros_like(xf)
        for e in range(Wd.shape[0]):
            y = H @ Wd[e] + bd[e]
            sel = (assign == e)[:, None]
            out = out + jnp.where(sel, probs[:, e:e + 1] * y, 0.0)
        return out.reshape(orig_shape)
    x = x + _L0_gnn_ref(_layernorm(x, axis=-1), adj, L0_gnn_W, L0_gnn_a_1, L0_gnn_a_2, L0_gnn_a_12, L0_gnn_W_1, L0_gnn_W_2)
    x = x + _L0_ffn_ref(_layernorm(x, axis=-1), L0_ffn_W1, L0_ffn_b1, L0_ffn_Wg, L0_ffn_bg, L0_ffn_Wd, L0_ffn_bd)
    return x

_drawn_inputs = setup_inputs


def setup_inputs(seed=0):
    import zlib

    import numpy as np

    out = dict(_drawn_inputs(seed))
    spreads = {'L0_ffn_b1': (0.0, 0.8), 'L0_ffn_bg': (0.0, 0.76), 'L0_ffn_bd': (0.0, 0.8)}
    factors = {'L0_gnn_a_2': 8.0, 'L0_ffn_W1': 8.0, 'L0_ffn_Wg': 8.0, 'L0_ffn_Wd': 8.0}
    for name, (base, spread) in spreads.items():
        noise = np.random.default_rng([zlib.crc32(name.encode()), seed]).standard_normal(out[name].shape)
        drawn = base * np.exp(spread * noise) if base else spread * noise
        out[name] = jnp.asarray(drawn.astype(out[name].dtype))
    for name, factor in factors.items():
        out[name] = (out[name] * factor).astype(out[name].dtype)
    return out
```

```python
from contextlib import ExitStack

import concourse.bass as bass
from concourse import mybir

F32 = mybir.dt.float32
I32 = mybir.dt.int32
BF16 = mybir.dt.bfloat16
ALU = mybir.AluOpType
ACT = mybir.ActivationFunctionType
AX = mybir.AxisListType

P = 128
TPG = 4
RING = 4
SLOPE = 0.2
NEG = 9.0e15
OPEN = 3.0e38
EPS = 1e-5
ROW = 132
PROB, TOKEN, MEAN, RSTD = 128, 129, 130, 131


class Group:

    def __init__(self, n, ring):
        self.n, self.ring = n, ring % RING
        self.two = self.ring % 2


def slots(eng, emit, n_groups, depth, peeled):
    looped = (n_groups - peeled) // RING * RING
    for t in range(peeled):
        emit(Group(t, t))
    with eng.Fori(peeled // RING, (peeled + looped) // RING) as k:
        for j in range(RING):
            emit(Group(k * RING + j, j))
    for t in range(peeled + looped, n_groups + depth):
        emit(Group(t, t))


def back(t, by, n_groups):
    n = t.n - by
    if isinstance(n, int) and not 0 <= n < n_groups:
        return None
    return Group(n, t.ring - by)


def after(eng, sem, g, ago=0, per=1, last=None):
    n = (g.n - ago + 1) * per
    if isinstance(n, int):
        if n <= 0:
            return
        if last is not None:
            n = min(n, last * per)
    eng.wait_ge(sem, n)


def build(nc, x, adj, g_w, g_a1, g_a2, g_a12, g_w1, g_w2, f_w1, f_b1, f_wg, f_bg, f_wd, f_bd, rows, out):
    NB = x.shape[0]
    C = x.shape[2]
    HID = f_w1.shape[1]
    NE = f_wd.shape[0]
    NCH = HID // P
    NG = NB // TPG
    N = TPG * P
    TOKENS = NB * P
    REGION = TOKENS + P
    NT = TOKENS // P + NE
    NQ = NT // TPG
    DEPTH1, PEEL1 = 6, 8
    DEPTH2, PEEL2 = 4, 8

    ctx = ExitStack()
    with ctx:
        def sb(name, shape, dt=F32):
            return ctx.enter_context(nc.sbuf_tensor(name, shape, dt))

        def sem(name):
            return ctx.enter_context(nc.semaphore(name))

        w_sb, a12_sb = sb("w_sb", [P, C]), sb("a12_sb", [P, C])
        a_sb = sb("a_sb", [P, 2])
        wT, a12T, a12wT = sb("wT", [P, C]), sb("a12T", [P, C]), sb("a12wT", [P, C])
        pair = sb("pair", [P, C])
        uv = sb("uv", [P, 2])
        w1g, w2g = sb("w1g", [P, C]), sb("w2g", [P, C])
        w1f = sb("w1f", [P, HID])
        b1f = sb("b1f", [P, NCH])
        wg = sb("wg", [P, NCH, NE])
        bg = sb("bg", [P, NE])
        wd = sb("wd", [P, NE * NCH * C])
        bd = sb("bd", [1, NE * C])
        ident = sb("ident", [P, P])
        ones_row = sb("ones_row", [1, P])
        before = sb("before", [P, P], BF16)
        ones_bf = sb("ones_bf", [P, P], BF16)
        ones_f = sb("ones_f", [P, P])
        half = sb("half", [P, TPG])
        first = sb("first", [P, NE])
        carry_i = sb("carry_i", [P, NE], I32)
        carry = sb("carry", [P, NE])
        region0 = sb("region0", [P, NE])
        part_f = sb("part_f", [P, 1])
        part_i = sb("part_i", [P, 1], I32)
        upto = sb("upto", [P, NE, NE])
        tile_i = sb("tile_i", [P, NT], I32)
        tile_no = sb("tile_no", [P, NT])
        padrow = sb("padrow", [P, ROW])
        tok_i = sb("tok_i", [P, TPG], I32)
        tok = sb("tok", [P, TPG])
        first_i = sb("first_i", [P, NE], I32)

        spare = sb("spare", [1, 256])
        turn = sb("turn", [1, RING])
        used_spare = [0]

        xb = sb("xb", [P, RING, TPG, C])
        adjb = sb("adjb", [P, 2, TPG, P], I32)
        maskb = sb("maskb", [P, 2, TPG, P])
        bn = sb("bn", [P, 2, TPG, 6])
        mv = sb("mv", [P, 2, TPG, 2])
        ve = sb("ve", [P, 2, TPG])
        rstd = sb("rstd", [P, 2, TPG])
        fn = sb("fn", [P, 2, TPG, C])
        fT = sb("fT", [P, RING, N])
        gT = sb("gT", [P, 2, N])
        f2 = sb("f2", [P, RING, TPG, C])
        vcol = sb("vcol", [P, 2, TPG])
        lg = sb("lg", [P, 2, TPG, P])
        relu = sb("relu", [P, 2, TPG, P])
        nmax = sb("nmax", [P, 2, TPG])
        pr = sb("pr", [P, 2, TPG, P])
        psumr = sb("psumr", [P, 2, TPG])
        rsum = sb("rsum", [P, 2, TPG])
        pT = sb("pT", [P, 2, N])
        ex = sb("ex", [P, 2, TPG, C])
        rr = sb("rr", [P, 2, TPG, C])
        rowb = sb("rowb", [P, RING, TPG, ROW])
        bn2 = sb("bn2", [P, 2, TPG, 6])
        ve2 = sb("ve2", [P, 2, TPG])
        xn2 = sb("xn2", [P, 2, TPG, C])
        xT = sb("xT", [P, 2, N])
        hT = sb("hT", [P, 2, NCH, N])
        gl = sb("gl", [P, 2, TPG, NE])
        gmx = sb("gmx", [P, 2, TPG])
        gd = sb("gd", [P, 2, TPG, NE])
        ge = sb("ge", [P, 2, TPG, NE])
        gs = sb("gs", [P, 2, TPG])
        hit = sb("hit", [P, 2, TPG, NE])
        hmx = sb("hmx", [P, 2, TPG])
        hot = sb("hot", [P, 2, TPG, NE], BF16)
        pos = sb("pos", [P, 2, TPG, NE])
        pos2 = sb("pos2", [P, 2, TPG, NE])
        dest = sb("dest", [P, 2, TPG])
        desti = sb("desti", [P, RING, TPG], I32)

        cnt = sb("cnt", [P, NE])
        cnti = sb("cnti", [P, NE], I32)
        cntj = sb("cntj", [P, NE], I32)
        ntile = sb("ntile", [P, NE])
        upn = sb("upn", [P, NE, NE])
        incl = sb("incl", [P, NE])
        past = sb("past", [P, NT, NE])
        past2 = sb("past2", [P, NT, NE])
        tex = sb("tex", [P, NT])
        tst = sb("tst", [P, NT])
        trow = sb("trow", [P, NT])
        trow2 = sb("trow2", [P, NT])
        row_tab = sb("row_tab", [P, NT], I32)
        wd_tab = sb("wd_tab", [P, NT], I32)
        padf = sb("padf", [P, NE])
        padi = sb("padi", [P, NE], I32)

        crow = rowb
        cxn, cxT, chT = xn2, xT, hT
        cout = xb

        ps = ctx.enter_context(nc.psum_tensor("ps", [P, 8, 512], F32))
        B_TR, B_G, B_L, B_F2, B_SM, B_H, B_HID = 0, 1, 2, 3, 4, 5, 6
        B_Y = 2
        ps_v = ps[:, B_SM, 0:TPG]
        ps_gate = ps[:, B_SM, 64:64 + TPG * NE].rearrange("p (t e) -> p t e", e=NE)
        ps_rank = ps[:, B_SM, 128:128 + TPG * NE].rearrange("p (t e) -> p t e", e=NE)
        ps_tot = ps[:, B_SM, 192:192 + NE]

        def bank(b):
            return ps[:, b, :].rearrange("p (t c) -> p t c", t=TPG)

        w_loaded = sem("w_loaded")
        consts = sem("consts")
        setup_pe, setup_dve = sem("setup_pe"), sem("setup_dve")
        x_in = [sem(f"x_in{i}") for i in range(RING)]
        adj_in = [sem(f"adj_in{i}") for i in range(2)]
        names = ["stats", "var_eps", "rstd_ok", "fn_ok", "fT_ps", "fT_ok", "g_ps", "gT_ok", "f2_ps", "f2_ok", "vcol_ok",
                 "lg_ps", "relu_ok", "mask_ok", "masked", "leaky_ok", "nmax_ok", "probs", "rsum_ok", "probs_n", "pT_ps", "pT_ok",
                 "hout_ps", "expm", "elu_neg", "elu_pos", "x2_ok", "bn_ok", "bn2_ok",
                 "stats2", "var_eps2", "rstd2_ok", "xn_ok", "xT_ps", "xT_ok", "hid_ps", "hid_ok",
                 "gate_ps", "gl_ok", "gmx_ok", "gd_ok", "gate_exp", "gs_ok", "prob_ok", "hit0", "hit1", "hmx_ok", "hot_ok",
                 "rank_ps", "pos_ok", "tok_ok", "tok_next", "carried", "pos_hot", "dest_ok", "desti_ok"]
        S = {n: sem(n) for n in names}
        sent = [sem(f"sent{i}") for i in range(2)]
        pads_sent = sem("pads_sent")
        pad0_sent = sem("pad0_sent")
        tab = sem("tab")
        pads_ready = sem("pads_ready")
        rows_in = [sem(f"rows_in{i}") for i in range(RING)]
        out_sent = [sem(f"out_sent{i}") for i in range(2)]
        C_ = {n: sem("c_" + n) for n in ["xn", "xT_ps", "xT", "hid_ps", "hid", "y_ps", "out", "turn"]}

        def hold(eng, *waits):
            waits = [w for w in waits if w]
            for s, n in waits:
                eng.wait_ge(s, n)
            if any(not isinstance(n, int) for _, n in waits):
                one = spare[:, used_spare[0]:used_spare[0] + 1]
                used_spare[0] += 1
                if eng.engine == mybir.EngineType.Pool:
                    nc.gpsimd.tensor_tensor(one, half[0:1, 0:1], half[0:1, 0:1], ALU.add)
                else:
                    nc.vector.memset(one, 0.0)

        def plain(eng, wait):
            if wait:
                eng.wait_ge(*wait)

        def of(sem_, g, ago=0, per=1):
            n = (g.n - ago + 1) * per
            return None if isinstance(n, int) and n <= 0 else (sem_, n)

        def landed(sem_, g, per, ago=0):
            if isinstance(g.n, int):
                n = ((g.n - g.two) // 2 + 1 - ago // 2) * 16 * per
                return (sem_, n) if n > 0 else None
            return (sem_, (g.n + (2 - g.two - ago)) * (8 * per))

        block = ctx.enter_context(nc.Block())
        x_g = x.rearrange("(g t) n c -> g n t c", t=TPG)
        adj_g = adj.rearrange("(g t) n m -> g n t m", t=TPG)
        out_rows = out.rearrange("b n c -> (b n) c")
        N_LOADS = 14

        @block.sync
        def _(sp):
            for dst, src in ((w_sb[:], g_w), (a12_sb[:], g_a12), (a_sb[:, 0:1], g_a1), (a_sb[:, 1:2], g_a2),
                             (w1g[:], g_w1), (w2g[:], g_w2), (w1f[:], f_w1),
                             (b1f[:], f_b1.rearrange("(h p) -> p h", p=P)),
                             (wg[:], f_wg.rearrange("(h p) e -> p h e", p=P)),
                             (bg[0:1, :], f_bg.rearrange("(o e) -> o e", o=1)),
                             (bd[:], f_bd.rearrange("(o e) c -> o (e c)", o=1))):
                sp.dma_start(dst, src, allow_slow_non_contiguous=True).then_inc(w_loaded, 16)
            sp.dma_start(wd[:].rearrange("p (e h c) -> p e h c", e=NE, h=NCH),
                         f_wd.rearrange("e (h p) c -> p e h c", p=P)).then_inc(w_loaded, 16)

            def load(t):
                g = back(t, 0, NG)
                if g is None:
                    return
                after(sp, S["elu_pos"], g, RING)
                sp.dma_start(xb[:, g.ring], x_g[g.n] if isinstance(g.n, int) else
                             x_g[bass.ds(g.n, 1)].rearrange("o n t c -> (o n) t c")).then_inc(x_in[g.ring], 16)
                after(sp, S["mask_ok"], g, 2)
                sp.dma_start(adjb[:, g.two], adj_g[g.n] if isinstance(g.n, int) else
                             adj_g[bass.ds(g.n, 1)].rearrange("o n t c -> (o n) t c")).then_inc(adj_in[g.two], 16)

            slots(sp, load, NG, 0, PEEL1)

            for s in sent:
                sp.wait_ge(s, 16 * TPG * NG // 2)
            sp.wait_ge(pads_sent, 16 * NE)
            sp.wait_ge(pad0_sent, 16)
            sp.wait_ge(tab, 14)

            def load_rows(t):
                q = back(t, 0, NQ)
                if q is None:
                    return
                plain(sp, landed(out_sent[q.two], q, TPG, RING))
                for b in range(TPG):
                    r = sp.value_load(row_tab[0:1, bass.ds(q.n * TPG + b, 1)], min_val=0, max_val=NE * REGION)
                    sp.dma_start(crow[:, q.ring, b, :], rows[bass.ds(r, P), :]).then_inc(rows_in[q.ring], 16)

            slots(sp, load_rows, NQ, 0, PEEL2)
            for i in range(2):
                sp.wait_ge(out_sent[i], 16 * TPG * NQ // 2)

        @block.gpsimd
        def _(pool):
            nc.gpsimd.memset(ident[:], 0.0).then_inc(consts, 1)
            nc.gpsimd.memset(before[:], 0.0).then_inc(consts, 1)
            nc.gpsimd.memset(ones_bf[:], 1.0).then_inc(consts, 1)
            nc.gpsimd.memset(ones_row[:], 1.0).then_inc(consts, 1)
            nc.gpsimd.memset(half[:], -0.5).then_inc(consts, 1)
            nc.gpsimd.memset(upto[:], 1.0).then_inc(consts, 1)
            nc.gpsimd.memset(padrow[:], 0.0).then_inc(consts, 1)
            nc.gpsimd.iota(first_i[:], pattern=[[-1, NE]], base=NE, channel_multiplier=0).then_inc(consts, 1)
            nc.gpsimd.iota(carry_i[:], pattern=[[REGION, NE]], base=0, channel_multiplier=0).then_inc(consts, 1)
            nc.gpsimd.iota(part_i[:], pattern=[[0, 1]], base=0, channel_multiplier=1).then_inc(consts, 1)
            nc.gpsimd.iota(tile_i[:], pattern=[[1, NT]], base=0, channel_multiplier=0).then_inc(consts, 1)
            nc.gpsimd.iota(tok_i[:], pattern=[[P, TPG]], base=0, channel_multiplier=1).then_inc(consts, 1)
            pool.wait_ge(consts, 12)
            nc.gpsimd.affine_select(out=ident[:], in_=ident[:], compare_op=ALU.not_equal, fill=1.0, base=0,
                                    pattern=[[-1, P]], channel_multiplier=1).then_inc(consts, 1)
            nc.gpsimd.affine_select(out=before[:], in_=before[:], compare_op=ALU.is_ge, fill=1.0, base=0,
                                    pattern=[[-1, P]], channel_multiplier=1).then_inc(consts, 1)
            nc.gpsimd.affine_select(out=upto[:], in_=upto[:], compare_op=ALU.is_ge, fill=0.0, base=0,
                                    pattern=[[1, NE], [-1, NE]], channel_multiplier=0).then_inc(consts, 1)
            nc.gpsimd.iota(padrow[:, TOKEN:TOKEN + 1].bitcast(I32), pattern=[[0, 1]], base=TOKENS,
                           channel_multiplier=0).then_inc(consts, 1)
            nc.gpsimd.tensor_copy(first[:], first_i[:]).then_inc(consts, 1)
            nc.gpsimd.tensor_copy(carry[:], carry_i[:]).then_inc(consts, 1)
            nc.gpsimd.tensor_copy(region0[:], carry_i[:]).then_inc(consts, 1)
            nc.gpsimd.tensor_copy(part_f[:], part_i[:]).then_inc(consts, 1)
            nc.gpsimd.tensor_copy(tile_no[:], tile_i[:]).then_inc(consts, 1)
            nc.gpsimd.tensor_copy(tok[:], tok_i[:]).then_inc(consts, 1)
            pool.wait_ge(consts, 22)
            pool.dma_start(rows[NE * REGION:NE * REGION + P, :], padrow[:]).then_inc(pad0_sent, 16)

            def mask(t):
                g = back(t, 1, NG)
                if g is None:
                    return
                hold(pool, landed(adj_in[g.two], g, 1), of(S["masked"], g, 2))
                nc.gpsimd.tensor_scalar(maskb[:, g.two], adjb[:, g.two], 0, OPEN, ALU.is_gt,
                                        ALU.mult).then_inc(S["mask_ok"], 1)

            def power(t, by, stats, var_eps, ve_, var_of, out_of, done, used):
                g = back(t, by, NG)
                if g is None:
                    return
                hold(pool, of(S[stats], g))
                nc.gpsimd.tensor_scalar(ve_[:, g.two], var_of(g), EPS, None, ALU.add).then_inc(S[var_eps], 1)
                hold(pool, of(S[var_eps], g), of(S[used], g, 2))
                nc.gpsimd.tensor_tensor(out_of(g), ve_[:, g.two], half[:], ALU.pow).then_inc(S[done], 1)

            def send(t):
                g = back(t, 6, NG)
                if g is None:
                    return
                hold(pool, of(S["x2_ok"], g), of(S["tok_next"], g, 1))
                nc.gpsimd.tensor_copy(rowb[:, g.ring, :, TOKEN].bitcast(I32), tok[:]).then_inc(S["tok_ok"], 1)
                hold(pool, of(S["tok_ok"], g))
                nc.gpsimd.tensor_scalar(tok[:], tok[:], float(N), None, ALU.add).then_inc(S["tok_next"], 1)
                hold(pool, of(S["desti_ok"], g), of(S["prob_ok"], g), of(S["rstd2_ok"], g),
                     landed(sent[g.two], g, TPG, 2))
                for b in range(TPG):
                    nc.gpsimd.indirect_dma_start(
                        rows[:, :], bass.IndirectOffsetOnAxis(desti[:, g.ring, b:b + 1], 0), rowb[:, g.ring, b, :], None,
                        bounds_check=NE * REGION - 1, oob_is_err=False).then_inc(sent[g.two], 16)

            def slot(t):
                mask(t)
                power(t, 0, "stats", "var_eps", ve, lambda g: mv[:, g.two, :, 1],
                      lambda g: rstd[:, g.two], "rstd_ok", "fn_ok")
                power(t, 4, "stats2", "var_eps2", ve2, lambda g: rowb[:, g.ring, :, RSTD],
                      lambda g: rowb[:, g.ring, :, RSTD], "rstd2_ok", "xn_ok")
                send(t)

            slots(pool, slot, NG, DEPTH1, PEEL1)
            pool.wait_ge(pads_ready, 2)
            for e in range(NE):
                nc.gpsimd.indirect_dma_start(
                    rows[:, :], bass.IndirectOffsetOnAxis(padi[:, e:e + 1], 0), padrow[:], None,
                    bounds_check=NE * REGION - 1, oob_is_err=False).then_inc(pads_sent, 16)

            def send_out(t):
                q = back(t, 4, NQ)
                if q is None:
                    return
                plain(pool, of(C_["out"], q))
                plain(pool, landed(out_sent[q.two], q, TPG, 2))
                nc.gpsimd.tensor_tensor(turn[:, q.ring:q.ring + 1], half[0:1, 0:1], half[0:1, 0:1],
                                        ALU.add).then_inc(C_["turn"], 1)
                for b in range(TPG):
                    nc.gpsimd.indirect_dma_start(
                        out_rows[:, :],
                        bass.IndirectOffsetOnAxis(crow[:, q.ring, b, TOKEN:TOKEN + 1].bitcast(I32), 0),
                        cout[:, q.ring, b, :], None,
                        bounds_check=TOKENS - 1, oob_is_err=False).then_inc(out_sent[q.two], 16)

            slots(pool, send_out, NQ, DEPTH2, PEEL2)

        @block.tensor
        def _(pe):
            pe.wait_ge(consts, 22)
            pe.wait_ge(w_loaded, 16 * 12)
            nc.tensor.transpose(ps[:, 0, 0:P], w_sb[:], ident[:])
            nc.tensor.transpose(ps[:, 0, P:2 * P], a12_sb[:], ident[:]).then_inc(setup_pe, 1)
            pe.wait_ge(setup_dve, 2)
            nc.tensor.matmul(ps[:, 1, 0:C], a12T[:], wT[:], start=True, stop=True)
            nc.tensor.matmul(ps[:, 1, 256:258], wT[:], a_sb[:], start=True, stop=True)
            nc.tensor.matmul(ps[:, 1, 320:320 + NE], ones_row[:], bg[0:1, :], start=True, stop=True).then_inc(setup_pe, 1)
            pe.wait_ge(setup_dve, 5)
            nc.tensor.matmul(ps[:, 2, 0:C], wT[:], a12wT[:], start=True, stop=True).then_inc(setup_pe, 1)
            pe.wait_ge(setup_dve, 6)

            def t_fT(t):
                g = back(t, 1, NG)
                if g is None:
                    return
                after(pe, S["fn_ok"], g)
                after(pe, S["xT_ok"], g, 4)
                after(pe, S["pT_ok"], g, 3)
                for b in range(TPG):
                    m = nc.tensor.transpose(bank(B_TR)[:, b, :], fn[:, g.two, b, :], ident[:])
                m.then_inc(S["fT_ps"], 1)

            def t_g(t):
                g = back(t, 1, NG)
                if g is None:
                    return
                after(pe, S["fT_ok"], g)
                after(pe, S["gT_ok"], g, 1)
                nc.tensor.matmul(ps[:, B_G, :], pair[:], fT[:, g.ring], start=True, stop=True).then_inc(S["g_ps"], 1)

            def t_f2(t):
                g = back(t, 1, NG)
                if g is None:
                    return
                after(pe, S["f2_ok"], g, 1)
                after(pe, S["gl_ok"], g, 5)
                for b in range(TPG):
                    f_b = fT[:, g.ring, b * P:(b + 1) * P]
                    nc.tensor.matmul(bank(B_F2)[:, b, :], f_b, w2g[:], start=True, stop=True)
                    m = nc.tensor.matmul(ps_v[:, b:b + 1], f_b, uv[:, 1:2], start=True, stop=True)
                m.then_inc(S["f2_ps"], 1)

            def t_lg(t):
                g = back(t, 2, NG)
                if g is None:
                    return
                after(pe, S["gT_ok"], g)
                after(pe, S["leaky_ok"], g, 1)
                for b in range(TPG):
                    m = nc.tensor.matmul(bank(B_L)[:, b, :], gT[:, g.two, b * P:(b + 1) * P],
                                         fT[:, g.ring, b * P:(b + 1) * P], start=True, stop=True)
                m.then_inc(S["lg_ps"], 1)

            def t_pT(t):
                g = back(t, 3, NG)
                if g is None:
                    return
                after(pe, S["probs_n"], g)
                after(pe, S["xT_ok"], g, 2)
                after(pe, S["fT_ok"], g, -2, last=NG)
                for b in range(TPG):
                    m = nc.tensor.transpose(bank(B_TR)[:, b, :], pr[:, g.two, b, :], ident[:])
                m.then_inc(S["pT_ps"], 1)

            def t_hout(t):
                g = back(t, 3, NG)
                if g is None:
                    return
                after(pe, S["pT_ok"], g)
                after(pe, S["f2_ok"], g)
                after(pe, S["elu_pos"], g, 1)
                after(pe, S["expm"], g, 1)
                for b in range(TPG):
                    nc.tensor.matmul(bank(B_H)[:, b, :], fT[:, g.ring, b * P:(b + 1) * P], w1g[:], start=True, stop=False)
                    m = nc.tensor.matmul(bank(B_H)[:, b, :], pT[:, g.two, b * P:(b + 1) * P], f2[:, g.ring, b, :],
                                         start=False, stop=True)
                m.then_inc(S["hout_ps"], 1)

            def t_xT(t):
                g = back(t, 5, NG)
                if g is None:
                    return
                after(pe, S["xn_ok"], g)
                after(pe, S["pT_ok"], g, -1, last=NG)
                for b in range(TPG):
                    m = nc.tensor.transpose(bank(B_TR)[:, b, :], xn2[:, g.two, b, :], ident[:])
                m.then_inc(S["xT_ps"], 1)

            def t_hid(t, chunks):
                g = back(t, 5, NG)
                if g is None:
                    return
                after(pe, S["xT_ok"], g)
                for h in chunks:
                    n = g.n * NCH + h - 1
                    if not (isinstance(n, int) and n <= 0):
                        pe.wait_ge(S["hid_ok"], n)
                    nc.tensor.matmul(ps[:, B_HID + h % 2, :], w1f[:, h * P:(h + 1) * P], xT[:, g.two],
                                     start=True, stop=True).then_inc(S["hid_ps"], 1)

            def t_gate(t):
                g = back(t, 5, NG)
                if g is None:
                    return
                after(pe, S["hid_ok"], g, 0, NCH)
                after(pe, S["pos_ok"], g, 1)
                after(pe, S["carried"], g, 1)
                after(pe, S["vcol_ok"], g, -4, last=NG)
                for b in range(TPG):
                    for h in range(NCH):
                        m = nc.tensor.matmul(ps_gate[:, b, :], hT[:, g.two, h, b * P:(b + 1) * P], wg[:, h, :],
                                             start=(h == 0), stop=(h == NCH - 1))
                m.then_inc(S["gate_ps"], 1)

            def t_rank(t):
                g = back(t, 6, NG)
                if g is None:
                    return
                after(pe, S["hot_ok"], g)
                after(pe, S["vcol_ok"], g, -5, last=NG)
                for b in range(TPG):
                    nc.tensor.matmul(ps_rank[:, b, :], before[:], hot[:, g.two, b, :], start=True, stop=(b == 0))
                    for a in range(b):
                        nc.tensor.matmul(ps_rank[:, b, :], ones_bf[:], hot[:, g.two, a, :], start=False,
                                         stop=(a == b - 1))
                for b in range(TPG):
                    m = nc.tensor.matmul(ps_tot, ones_bf[:], hot[:, g.two, b, :], start=(b == 0), stop=(b == TPG - 1))
                m.then_inc(S["rank_ps"], 1)

            def slot(t):
                t_xT(t)
                t_lg(t)
                t_hid(t, (0, 1))
                t_fT(t)
                t_g(t)
                t_pT(t)
                t_hid(t, (2, 3))
                t_f2(t)
                t_hout(t)
                t_rank(t)
                t_gate(t)

            slots(pe, slot, NG, DEPTH1, PEEL1)

            pe.wait_ge(tab, 14)

            def c_xT(t):
                q = back(t, 1, NQ)
                if q is None:
                    return
                after(pe, C_["xn"], q)
                after(pe, C_["xT"], q, 1)
                for b in range(TPG):
                    m = nc.tensor.transpose(bank(B_TR)[:, b, :], cxn[:, q.two, b, :], ident[:])
                m.then_inc(C_["xT_ps"], 1)

            def c_hid(t, chunks):
                q = back(t, 2, NQ)
                if q is None:
                    return
                after(pe, C_["xT"], q)
                for h in chunks:
                    n = q.n * NCH + h - 1
                    if not (isinstance(n, int) and n <= 0):
                        pe.wait_ge(C_["hid"], n)
                    nc.tensor.matmul(ps[:, B_HID + h % 2, :], w1f[:, h * P:(h + 1) * P], cxT[:, q.two],
                                     start=True, stop=True).then_inc(C_["hid_ps"], 1)

            def c_y(t, tiles):
                q = back(t, 3, NQ)
                if q is None:
                    return
                after(pe, C_["hid"], q, 0, NCH)
                after(pe, C_["out"], q, 2)
                for b in tiles:
                    w = pe.value_load(wd_tab[0:1, bass.ds(q.n * TPG + b, 1)], min_val=0, max_val=NE - 1)
                    nc.tensor.matmul(bank(B_Y + q.two)[:, b, :], ones_row[:], bd[0:1, bass.ds(w * C, C)],
                                     start=True, stop=False)
                    for h in range(NCH):
                        m = nc.tensor.matmul(bank(B_Y + q.two)[:, b, :], chT[:, q.two, h, b * P:(b + 1) * P],
                                             wd[:, bass.ds(w * (NCH * C) + h * C, C)], start=False,
                                             stop=(h == NCH - 1))
                    m.then_inc(C_["y_ps"], 1)

            def slot_c(t):
                c_y(t, (0, 1))
                c_hid(t, (0, 1))
                c_xT(t)
                c_y(t, (2, 3))
                c_hid(t, (2, 3))

            slots(pe, slot_c, NQ, DEPTH2, PEEL2)

        @block.scalar
        def _(act):
            act.wait_ge(setup_dve, 6)

            def a_fT(t):
                g = back(t, 1, NG)
                if g is None:
                    return
                after(act, S["fT_ps"], g)
                after(act, S["hout_ps"], g, RING)
                nc.scalar.copy(fT[:, g.ring], ps[:, B_TR, :]).then_inc(S["fT_ok"], 1)

            def a_gT(t):
                g = back(t, 1, NG)
                if g is None:
                    return
                after(act, S["g_ps"], g)
                after(act, S["lg_ps"], g, 2)
                nc.scalar.activation(gT[:, g.two], ps[:, B_G, :], ACT.Identity, bias=uv[:, 0:1]).then_inc(S["gT_ok"], 1)

            def a_relu(t):
                g = back(t, 2, NG)
                if g is None:
                    return
                after(act, S["lg_ps"], g)
                after(act, S["vcol_ok"], g)
                after(act, S["leaky_ok"], g, 2)
                for b in range(TPG):
                    m = nc.scalar.activation(relu[:, g.two, b, :], bank(B_L)[:, b, :], ACT.Relu,
                                             bias=vcol[:, g.two, b:b + 1], scale=1.0 - SLOPE)
                m.then_inc(S["relu_ok"], 1)

            def a_exp(t):
                g = back(t, 2, NG)
                if g is None:
                    return
                after(act, S["nmax_ok"], g)
                after(act, S["pT_ps"], g, 2)
                after(act, S["rsum_ok"], g, 2)
                for b in range(TPG):
                    nc.scalar.activation(pr[:, g.two, b, :], lg[:, g.two, b, :], ACT.Exp, bias=nmax[:, g.two, b:b + 1],
                                         accum_out=psumr[:, g.two, b:b + 1]).then_inc(S["probs"], 1)

            def a_expm(t):
                g = back(t, 3, NG)
                if g is None:
                    return
                after(act, S["hout_ps"], g)
                after(act, S["x2_ok"], g, 2)
                nc.scalar.activation(ex[:, g.two], bank(B_H), ACT.Exp).then_inc(S["expm"], 1)

            def a_xT(t):
                g = back(t, 5, NG)
                if g is None:
                    return
                after(act, S["xT_ps"], g)
                after(act, S["hid_ps"], g, 2, NCH)
                nc.scalar.copy(xT[:, g.two], ps[:, B_TR, :]).then_inc(S["xT_ok"], 1)

            def a_gelu(t, chunks):
                g = back(t, 5, NG)
                if g is None:
                    return
                after(act, S["gate_ps"], g, 2)
                for h in chunks:
                    act.wait_ge(S["hid_ps"], g.n * NCH + (h + 1))
                    nc.scalar.activation(hT[:, g.two, h, :], ps[:, B_HID + h % 2, :], ACT.Gelu,
                                         bias=b1f[:, h:h + 1]).then_inc(S["hid_ok"], 1)

            def a_gate(t):
                g = back(t, 6, NG)
                if g is None:
                    return
                after(act, S["gd_ok"], g)
                after(act, S["gs_ok"], g, 2)
                nc.scalar.activation(ge[:, g.two], gd[:, g.two], ACT.Exp).then_inc(S["gate_exp"], 1)

            def slot(t):
                a_xT(t)
                a_gelu(t, (0,))
                a_fT(t)
                a_relu(t)
                a_gelu(t, (1, 2, 3))
                a_gT(t)
                a_exp(t)
                a_gate(t)
                a_expm(t)

            slots(act, slot, NG, DEPTH1, PEEL1)

            def c_gelu(t):
                q = back(t, 2, NQ)
                if q is None:
                    return
                after(act, C_["y_ps"], q, 2, TPG)
                for h in range(NCH):
                    act.wait_ge(C_["hid_ps"], q.n * NCH + (h + 1))
                    nc.scalar.activation(chT[:, q.two, h, :], ps[:, B_HID + h % 2, :], ACT.Gelu,
                                         bias=b1f[:, h:h + 1]).then_inc(C_["hid"], 1)

            slots(act, c_gelu, NQ, DEPTH2, PEEL2)

        @block.vector
        def _(dve):
            V = nc.vector
            dve.wait_ge(setup_pe, 1)
            V.tensor_copy(wT[:], ps[:, 0, 0:P]).then_inc(setup_dve, 1)
            V.tensor_copy(a12T[:], ps[:, 0, P:2 * P]).then_inc(setup_dve, 1)
            dve.wait_ge(setup_pe, 2)
            V.tensor_copy(a12wT[:], ps[:, 1, 0:C]).then_inc(setup_dve, 1)
            V.tensor_copy(uv[:], ps[:, 1, 256:258]).then_inc(setup_dve, 1)
            V.tensor_copy(bg[:], ps[:, 1, 320:320 + NE]).then_inc(setup_dve, 1)
            dve.wait_ge(setup_pe, 3)
            V.tensor_copy(pair[:], ps[:, 2, 0:C]).then_inc(setup_dve, 1)
            dve.wait_ge(consts, 22)
            dve.wait_ge(setup_dve, 6)

            def x_ready(g):
                if isinstance(g.n, int):
                    dve.wait_ge(x_in[g.ring], 16 * (g.n // RING + 1))
                else:
                    dve.wait_ge(x_in[g.ring], (g.n + (RING - g.ring)) * (16 // RING))

            def d_stats(t):
                g = back(t, 0, NG)
                if g is None:
                    return
                x_ready(g)
                after(dve, S["var_eps"], g, 2)
                for b in range(TPG):
                    m = V.bn_stats(bn[:, g.two, b, :], xb[:, g.ring, b, :])
                m.then_inc(S["bn_ok"], 1)
                hold(dve, of(S["bn_ok"], g))
                for b in range(TPG):
                    m = V.bn_aggr(mv[:, g.two, b, :], bn[:, g.two, b, :])
                m.then_inc(S["stats"], 1)

            def d_norm(t):
                g = back(t, 1, NG)
                if g is None:
                    return
                after(dve, S["rstd_ok"], g)
                after(dve, S["fT_ps"], g, 2)
                for b in range(TPG):
                    m = V.tensor_scalar(fn[:, g.two, b, :], xb[:, g.ring, b, :], mv[:, g.two, b, 0:1],
                                        rstd[:, g.two, b:b + 1], ALU.subtract, ALU.mult)
                m.then_inc(S["fn_ok"], 1)

            def d_f2(t):
                g = back(t, 1, NG)
                if g is None:
                    return
                after(dve, S["f2_ps"], g)
                after(dve, S["relu_ok"], g, 2)
                V.tensor_scalar(vcol[:, g.two], ps_v, 1.0 - SLOPE, None, ALU.mult).then_inc(S["vcol_ok"], 1)
                after(dve, S["hout_ps"], g, RING)
                V.tensor_copy(f2[:, g.ring], bank(B_F2)).then_inc(S["f2_ok"], 1)

            def d_mask(t):
                g = back(t, 2, NG)
                if g is None:
                    return
                after(dve, S["relu_ok"], g)
                after(dve, S["probs"], g, 2, TPG)
                V.scalar_tensor_tensor(lg[:, g.two], bank(B_L), SLOPE, relu[:, g.two], ALU.mult,
                                       ALU.add).then_inc(S["leaky_ok"], 1)
                after(dve, S["leaky_ok"], g)
                after(dve, S["mask_ok"], g)
                V.scalar_tensor_tensor(lg[:, g.two], maskb[:, g.two], NEG, lg[:, g.two], ALU.subtract,
                                       ALU.min).then_inc(S["masked"], 1)
                after(dve, S["masked"], g)
                after(dve, S["probs"], g, 2, TPG)
                V.tensor_reduce(nmax[:, g.two], lg[:, g.two], AX.X, ALU.max, negate=True).then_inc(S["nmax_ok"], 1)

            def d_probs(t):
                g = back(t, 3, NG)
                if g is None:
                    return
                after(dve, S["probs"], g, 0, TPG)
                V.reciprocal(rsum[:, g.two], psumr[:, g.two]).then_inc(S["rsum_ok"], 1)
                after(dve, S["rsum_ok"], g)
                for b in range(TPG):
                    m = V.tensor_scalar(pr[:, g.two, b, :], pr[:, g.two, b, :], rsum[:, g.two, b:b + 1], None, ALU.mult)
                m.then_inc(S["probs_n"], 1)

            def d_pT(t):
                g = back(t, 3, NG)
                if g is None:
                    return
                after(dve, S["pT_ps"], g)
                after(dve, S["hout_ps"], g, 2)
                V.tensor_copy(pT[:, g.two], ps[:, B_TR, :]).then_inc(S["pT_ok"], 1)

            def d_elu(t):
                g = back(t, 3, NG)
                if g is None:
                    return
                after(dve, S["hout_ps"], g)
                after(dve, S["x2_ok"], g, 2)
                after(dve, S["expm"], g)
                V.scalar_tensor_tensor(rr[:, g.two], bank(B_H), 0.0, xb[:, g.ring], ALU.max,
                                       ALU.add).then_inc(S["elu_pos"], 1)
                V.tensor_scalar(ex[:, g.two], ex[:, g.two], 1.0, -1.0, ALU.min, ALU.add).then_inc(S["elu_neg"], 1)
                after(dve, S["elu_pos"], g)
                after(dve, S["elu_neg"], g)
                plain(dve, landed(sent[g.two], g, TPG, RING))
                V.tensor_tensor(rowb[:, g.ring, :, 0:C], ex[:, g.two], rr[:, g.two], ALU.add).then_inc(S["x2_ok"], 1)

            def d_stats2(t):
                g = back(t, 4, NG)
                if g is None:
                    return
                after(dve, S["x2_ok"], g)
                for b in range(TPG):
                    m = V.bn_stats(bn2[:, g.two, b, :], rowb[:, g.ring, b, 0:C])
                m.then_inc(S["bn2_ok"], 1)
                hold(dve, of(S["bn2_ok"], g), of(S["var_eps2"], g, 2))
                for b in range(TPG):
                    m = V.bn_aggr(rowb[:, g.ring, b, MEAN:MEAN + 2], bn2[:, g.two, b, :])
                m.then_inc(S["stats2"], 1)

            def d_norm2(t):
                g = back(t, 5, NG)
                if g is None:
                    return
                after(dve, S["rstd2_ok"], g)
                after(dve, S["xT_ps"], g, 2)
                for b in range(TPG):
                    m = V.tensor_scalar(xn2[:, g.two, b, :], rowb[:, g.ring, b, 0:C], rowb[:, g.ring, b, MEAN:MEAN + 1],
                                        rowb[:, g.ring, b, RSTD:RSTD + 1], ALU.subtract, ALU.mult)
                m.then_inc(S["xn_ok"], 1)

            def wide(v):
                return v.unsqueeze(2).to_broadcast([P, TPG, NE])

            def d_gate(t):
                g = back(t, 6, NG)
                if g is None:
                    return
                after(dve, S["gate_ps"], g)
                V.tensor_tensor(gl[:, g.two], ps_gate, bg[:].unsqueeze(1).to_broadcast([P, TPG, NE]),
                                ALU.add).then_inc(S["gl_ok"], 1)
                after(dve, S["gl_ok"], g)
                V.tensor_reduce(gmx[:, g.two], gl[:, g.two], AX.X, ALU.max).then_inc(S["gmx_ok"], 1)
                after(dve, S["gmx_ok"], g)
                after(dve, S["gate_exp"], g, 2)
                V.tensor_tensor(gd[:, g.two], gl[:, g.two], wide(gmx[:, g.two]), ALU.subtract).then_inc(S["gd_ok"], 1)
                V.tensor_tensor(hit[:, g.two], gl[:, g.two], wide(gmx[:, g.two]), ALU.is_equal).then_inc(S["hit0"], 1)
                after(dve, S["hit0"], g)
                V.tensor_tensor(hit[:, g.two], hit[:, g.two], first[:].unsqueeze(1).to_broadcast([P, TPG, NE]),
                                ALU.mult).then_inc(S["hit1"], 1)
                after(dve, S["hit1"], g)
                V.tensor_reduce(hmx[:, g.two], hit[:, g.two], AX.X, ALU.max).then_inc(S["hmx_ok"], 1)
                after(dve, S["hmx_ok"], g)
                after(dve, S["rank_ps"], g, 2)
                V.tensor_tensor(hot[:, g.two], hit[:, g.two], wide(hmx[:, g.two]), ALU.is_equal).then_inc(S["hot_ok"], 1)

            def d_route(t):
                g = back(t, 6, NG)
                if g is None:
                    return
                after(dve, S["gate_exp"], g)
                V.tensor_reduce(gs[:, g.two], ge[:, g.two], AX.X, ALU.add).then_inc(S["gs_ok"], 1)
                after(dve, S["gs_ok"], g)
                V.reciprocal(rowb[:, g.ring, :, PROB], gs[:, g.two]).then_inc(S["prob_ok"], 1)
                after(dve, S["rank_ps"], g)
                if not (isinstance(g.n, int) and g.n == 0):
                    after(dve, S["carried"], g, 1)
                V.tensor_tensor(pos[:, g.two], ps_rank, carry[:].unsqueeze(1).to_broadcast([P, TPG, NE]),
                                ALU.add).then_inc(S["pos_ok"], 1)
                after(dve, S["pos_ok"], g)
                V.tensor_tensor(carry[:], ps_tot, carry[:], ALU.add).then_inc(S["carried"], 1)
                V.tensor_tensor(pos2[:, g.two], pos[:, g.two], hot[:, g.two], ALU.mult).then_inc(S["pos_hot"], 1)
                after(dve, S["pos_hot"], g)
                V.tensor_reduce(dest[:, g.two], pos2[:, g.two], AX.X, ALU.add).then_inc(S["dest_ok"], 1)
                after(dve, S["dest_ok"], g)
                V.tensor_copy(desti[:, g.ring], dest[:, g.two]).then_inc(S["desti_ok"], 1)

            def slot(t):
                d_norm2(t)
                d_norm(t)
                d_gate(t)
                d_probs(t)
                d_stats(t)
                d_pT(t)
                d_mask(t)
                d_f2(t)
                d_route(t)
                d_stats2(t)
                d_elu(t)

            slots(dve, slot, NG, DEPTH1, PEEL1)

            done = [0]

            def step(ins):
                done[0] += 1
                ins.then_inc(tab, 1)
                dve.wait_ge(tab, done[0])

            dve.wait_ge(S["carried"], NG)
            V.tensor_scalar(padf[:], carry[:], part_f[:, 0:1], None, ALU.add).then_inc(pads_ready, 1)
            dve.wait_ge(pads_ready, 1)
            V.tensor_copy(padi[:], padf[:]).then_inc(pads_ready, 1)
            step(V.tensor_tensor(cnt[:], carry[:], region0[:], ALU.subtract))
            step(V.tensor_scalar(cnti[:], cnt[:], float(P - 1), None, ALU.add))
            step(V.tensor_scalar(cntj[:], cnti[:], 7, None, ALU.arith_shift_right))
            step(V.tensor_copy(ntile[:], cntj[:]))
            step(V.tensor_tensor(upn[:], upto[:], ntile[:].unsqueeze(1).to_broadcast([P, NE, NE]), ALU.mult))
            step(V.tensor_reduce(incl[:], upn[:], AX.X, ALU.add))
            step(V.tensor_tensor(past[:], tile_no[:].unsqueeze(2).to_broadcast([P, NT, NE]),
                                 incl[:].unsqueeze(1).to_broadcast([P, NT, NE]), ALU.is_ge))
            step(V.tensor_reduce(tex[:], past[:], AX.X, ALU.add))
            step(V.tensor_tensor(past2[:], past[:], ntile[:].unsqueeze(1).to_broadcast([P, NT, NE]), ALU.mult))
            step(V.tensor_reduce(tst[:], past2[:], AX.X, ALU.add))
            step(V.tensor_tensor(trow[:], tile_no[:], tst[:], ALU.subtract))
            step(V.scalar_tensor_tensor(trow2[:], tex[:], float(REGION // P), trow[:], ALU.mult, ALU.add))
            step(V.tensor_scalar(row_tab[:], trow2[:], float(P), float(NE * REGION), ALU.mult, ALU.min))
            step(V.tensor_scalar(wd_tab[:], tex[:], float(NE - 1), None, ALU.min))

            def c_norm(t):
                q = back(t, 0, NQ)
                if q is None:
                    return
                if isinstance(q.n, int):
                    dve.wait_ge(rows_in[q.ring], 16 * TPG * (q.n // RING + 1))
                else:
                    dve.wait_ge(rows_in[q.ring], (q.n + (RING - q.ring)) * (16 * TPG // RING))
                after(dve, C_["xT_ps"], q, 2)
                for b in range(TPG):
                    m = V.tensor_scalar(cxn[:, q.two, b, :], crow[:, q.ring, b, 0:C], crow[:, q.ring, b, MEAN:MEAN + 1],
                                        crow[:, q.ring, b, RSTD:RSTD + 1], ALU.subtract, ALU.mult)
                m.then_inc(C_["xn"], 1)

            def c_xT(t):
                q = back(t, 1, NQ)
                if q is None:
                    return
                after(dve, C_["xT_ps"], q)
                after(dve, C_["hid_ps"], q, 2, NCH)
                V.tensor_copy(cxT[:, q.two], ps[:, B_TR, :]).then_inc(C_["xT"], 1)

            def c_out(t):
                q = back(t, 3, NQ)
                if q is None:
                    return
                plain(dve, landed(out_sent[q.two], q, TPG, RING))
                plain(dve, of(C_["turn"], q, RING))
                after(dve, C_["y_ps"], q, 0, TPG)
                for b in range(TPG):
                    m = V.scalar_tensor_tensor(cout[:, q.ring, b, :], bank(B_Y + q.two)[:, b, :],
                                               crow[:, q.ring, b, PROB:PROB + 1], crow[:, q.ring, b, 0:C],
                                               ALU.mult, ALU.add)
                m.then_inc(C_["out"], 1)

            def slot_c(t):
                c_norm(t)
                c_xT(t)
                c_out(t)

            slots(dve, slot_c, NQ, DEPTH2, PEEL2)


INPUTS = ["x", "adj", "L0_gnn_W", "L0_gnn_a_1", "L0_gnn_a_2", "L0_gnn_a_12", "L0_gnn_W_1", "L0_gnn_W_2",
          "L0_ffn_W1", "L0_ffn_b1", "L0_ffn_Wg", "L0_ffn_bg", "L0_ffn_Wd", "L0_ffn_bd"]


def kernel(**inputs):
    import numpy as np
    import concourse.bacc as bacc
    from concourse.bass_utils import run_bass_kernel_spmd

    nc = bacc.Bacc("TRN2", target_bir_lowering=False, num_devices=1)
    arrays, args = {}, []
    for name in INPUTS:
        a = np.ascontiguousarray(inputs[name])
        arrays[name] = a
        args.append(nc.dram_tensor(name, a.shape, mybir.dt.from_np(a.dtype), kind="ExternalInput").ap())
    nb, n, _ = inputs["x"].shape
    ne = inputs["L0_ffn_Wd"].shape[0]
    rows = nc.dram_tensor("rows", (ne * (nb * n + P) + P, ROW), F32).ap()
    out = nc.dram_tensor("out", inputs["x"].shape, F32, kind="ExternalOutput").ap()
    build(nc, *args, rows, out)
    return run_bass_kernel_spmd(nc, [arrays], core_ids=[0]).results[0]["out"]
```

```python
from contextlib import ExitStack

import concourse.bass as bass
from concourse import mybir

F32 = mybir.dt.float32
I32 = mybir.dt.int32
BF16 = mybir.dt.bfloat16
F32R = mybir.dt.float32r
ALU = mybir.AluOpType
ACT = mybir.ActivationFunctionType
AX = mybir.AxisListType

QUAD = 32
P = 128
TPG = 4
RING = 4
SLOPE = 0.2
NEG = -9.0e15
OPEN = 1.0e30
EPS = 1e-5
ROW = 132
PROB, TOKEN, MEAN, RSTD = 128, 129, 130, 131


class Group:

    def __init__(self, n, ring):
        self.n, self.ring = n, ring % RING
        self.two = self.ring % 2


def slots(eng, emit, n_groups, depth, peeled):
    looped = (n_groups - peeled) // RING * RING
    for t in range(peeled):
        emit(Group(t, t))
    with eng.Fori(peeled // RING, (peeled + looped) // RING) as k:
        for j in range(RING):
            emit(Group(k * RING + j, j))
    for t in range(peeled + looped, n_groups + depth):
        emit(Group(t, t))


def back(t, by, n_groups):
    n = t.n - by
    if isinstance(n, int) and not 0 <= n < n_groups:
        return None
    return Group(n, t.ring - by)


def after(eng, sem, g, ago=0, per=1, last=None):
    n = (g.n - ago + 1) * per
    if isinstance(n, int):
        if n <= 0:
            return
        if last is not None:
            n = min(n, last * per)
    eng.wait_ge(sem, n)


def build(nc, x, adj, g_w, g_a1, g_a2, g_a12, g_w1, g_w2, f_w1, f_b1, f_wg, f_bg, f_wd, f_bd, rows, out):
    NB = x.shape[0]
    C = x.shape[2]
    HID = f_w1.shape[1]
    NE = f_wd.shape[0]
    NCH = HID // P
    NG = NB // TPG
    N = TPG * P
    TOKENS = NB * P
    REGION = TOKENS + P
    NT = TOKENS // P + NE
    NQ = NT // TPG
    DEPTH1, PEEL1 = 7, 12
    DEPTH2, PEEL2 = 4, 8

    ctx = ExitStack()
    with ctx:
        def sb(name, shape, dt=F32):
            return ctx.enter_context(nc.sbuf_tensor(name, shape, dt))

        def sem(name):
            return ctx.enter_context(nc.semaphore(name))

        w_sb, a12_sb = sb("w_sb", [P, C]), sb("a12_sb", [P, C])
        a_sb = sb("a_sb", [P, 2])
        wT, a12T, a12wT = sb("wT", [P, C]), sb("a12T", [P, C]), sb("a12wT", [P, C])
        pair = sb("pair", [P, C])
        uv = sb("uv", [P, 2])
        w1g = sb("w1g", [P, C])
        w2v = sb("w2v", [P, C + 1])
        w1f = sb("w1f", [P, HID])
        w1_hi, w1_lo = sb("w1_hi", [P, HID], F32R), sb("w1_lo", [P, HID], F32R)
        b1f = sb("b1f", [P, NCH])
        wg = sb("wg", [P, NCH, QUAD])
        pick = sb("pick", [P, NE])
        bg = sb("bg", [P, NE])
        wd = sb("wd", [P, NE * NCH * C])
        bd = sb("bd", [3, NE * C])
        bd_rest = sb("bd_rest", [3, NE * C])
        bd_hi, bd_mid = sb("bd_hi", [3, NE * C], BF16), sb("bd_mid", [3, NE * C], BF16)
        bd_low, bd_some = sb("bd_low", [3, NE * C], BF16), sb("bd_some", [3, NE * C], BF16)
        bd3 = sb("bd3", [3, NE * C], BF16)
        ident = sb("ident", [P, P])
        ones_row = sb("ones_row", [1, P])
        before = sb("before", [P, P], BF16)
        ones_bf = sb("ones_bf", [P, P], BF16)
        ones_f = sb("ones_f", [P, P])
        half = sb("half", [P, TPG])
        first = sb("first", [P, NE])
        carry_i = sb("carry_i", [P, NE], I32)
        carry = sb("carry", [P, NE])
        region0 = sb("region0", [P, NE])
        part_f = sb("part_f", [P, 1])
        part_i = sb("part_i", [P, 1], I32)
        upto = sb("upto", [P, NE, NE])
        tile_i = sb("tile_i", [P, NT], I32)
        tile_no = sb("tile_no", [P, NT])
        padrow = sb("padrow", [P, ROW])
        tok_i = sb("tok_i", [P, TPG], I32)
        tok = sb("tok", [P, TPG])
        first_i = sb("first_i", [P, NE], I32)

        spare = sb("spare", [1, 256])
        turn = sb("turn", [1, RING])
        used_spare = [0]

        xb = sb("xb", [P, RING, TPG, C])
        adjb = sb("adjb", [P, 2, TPG, P], I32)
        maskb = sb("maskb", [P, 2, TPG, P])
        bn = sb("bn", [P, 2, TPG, 6])
        mv = sb("mv", [P, 2, TPG, 2])
        ve = sb("ve", [P, 2, TPG])
        rstd = sb("rstd", [P, 2, TPG])
        fn = sb("fn", [P, 2, TPG, C])
        fT = sb("fT", [P, RING, N])
        gT = sb("gT", [P, 2, N])
        f2 = sb("f2", [P, RING, TPG, C])
        vcol = sb("vcol", [P, 2, TPG])
        lg = sb("lg", [P, 2, TPG, P])
        relu = sb("relu", [P, 2, TPG, P])
        nmax = sb("nmax", [P, 2, TPG])
        pr = sb("pr", [P, 2, TPG, P])
        psumr = sb("psumr", [P, 2, TPG])
        rsum = sb("rsum", [P, 2, TPG])
        pT = sb("pT", [P, 2, N])
        ex = sb("ex", [P, 2, TPG, C])
        rr = sb("rr", [P, 2, TPG, C])
        rowb = sb("rowb", [P, RING, TPG, ROW])
        bn2 = sb("bn2", [P, 2, TPG, 6])
        ve2 = sb("ve2", [P, 2, TPG])
        xn2 = sb("xn2", [P, 2, TPG, C])
        xT = sb("xT", [P, 2, N])
        hT = sb("hT", [P, 2, NCH, N])
        gS = sb("gS", [P, 2, N])
        gl = sb("gl", [P, 2, TPG, NE])
        gmx = sb("gmx", [P, 2, TPG])
        gd = sb("gd", [P, 2, TPG, NE])
        ge = sb("ge", [P, 2, TPG, NE])
        gs = sb("gs", [P, 2, TPG])
        hit = sb("hit", [P, 2, TPG, NE])
        hmx = sb("hmx", [P, 2, TPG])
        hot = sb("hot", [P, 2, TPG, NE], BF16)
        pos = sb("pos", [P, 2, TPG, NE])
        pos2 = sb("pos2", [P, 2, TPG, NE])
        dest = sb("dest", [P, 2, TPG])
        desti = sb("desti", [P, RING, TPG], I32)

        cnt = sb("cnt", [P, NE])
        cnti = sb("cnti", [P, NE], I32)
        cntj = sb("cntj", [P, NE], I32)
        ntile = sb("ntile", [P, NE])
        upn = sb("upn", [P, NE, NE])
        incl = sb("incl", [P, NE])
        past = sb("past", [P, NT, NE])
        past2 = sb("past2", [P, NT, NE])
        tex = sb("tex", [P, NT])
        tst = sb("tst", [P, NT])
        trow = sb("trow", [P, NT])
        trow2 = sb("trow2", [P, NT])
        row_tab = sb("row_tab", [P, NT], I32)
        wd_tab = sb("wd_tab", [P, NT], I32)
        padf = sb("padf", [P, NE])
        padi = sb("padi", [P, NE], I32)

        crow = rowb
        cxn, chT = xn2, hT
        cx_hi, cx_lo = sb("cx_hi", [P, 2, N], F32R), sb("cx_lo", [P, 2, N], F32R)
        cout = xb
        ctok = desti

        ps = ctx.enter_context(nc.psum_tensor("ps", [P, 8, 512], F32))
        B_TR, B_G, B_L, B_F2, B_SM, B_H, B_HID = 0, 1, 2, 3, 4, 5, 6
        B_Y = 2
        F2_IN = 3
        ps_f2 = ps[:, B_F2, 0:F2_IN * (C + 1)].rearrange("p (t c) -> p t c", t=F2_IN)
        ps_f2b = ps[:, B_SM, 256:256 + C + 1].rearrange("p (t c) -> p t c", t=1)
        ps_gate = ps[:, B_SM, 64:64 + TPG * NE].rearrange("p (t e) -> p t e", e=NE)
        ps_rank = ps[:, B_SM, 128:128 + TPG * NE].rearrange("p (t e) -> p t e", e=NE)
        ps_tot = ps[:, B_SM, 192:192 + NE]

        def bank(b):
            return ps[:, b, :].rearrange("p (t c) -> p t c", t=TPG)

        w_loaded, bd_loaded, wd_loaded = sem("w_loaded"), sem("bd_loaded"), sem("wd_loaded")
        parts = sem("parts")
        consts = sem("consts")
        setup_pe, setup_dve = sem("setup_pe"), sem("setup_dve")
        x_in = [sem(f"x_in{i}") for i in range(RING)]
        adj_in = [sem(f"adj_in{i}") for i in range(2)]
        names = ["stats", "var_eps", "rstd_ok", "fn_ok", "fT_ps", "fT_ok", "g_ps", "gT_ok", "f2_ps", "f2_ok", "vcol_ok",
                 "lg_ps", "relu_ok", "mask_ok", "masked", "leaky_ok", "nmax_ok", "probs", "rsum_ok", "probs_n", "pT_ps", "pT_ok",
                 "hout_ps", "expm", "elu_neg", "elu_pos", "x2_ok", "bn_ok", "bn2_ok",
                 "stats2", "var_eps2", "rstd2_ok", "xn_ok", "xT_ps", "xT_ok", "hid_ps", "hid_ok",
                 "gcol_ps", "gS_ok", "gate_ps", "gl_ok", "gmx_ok", "gd_ok", "gate_exp", "gs_ok", "prob_ok", "hit0", "hit1", "hmx_ok", "hot_ok",
                 "rank_ps", "pos_ok", "tok_ok", "tok_next", "carried", "pos_hot", "dest_ok", "desti_ok"]
        S = {n: sem(n) for n in names}
        sent = [sem(f"sent{i}") for i in range(2)]
        pads_sent = sem("pads_sent")
        pad0_sent = sem("pad0_sent")
        tab = sem("tab")
        pads_ready = sem("pads_ready")
        rows_in = [sem(f"rows_in{i}") for i in range(RING)]
        out_sent = [sem(f"out_sent{i}") for i in range(2)]
        C_ = {n: sem("c_" + n) for n in ["xn", "xT_ps", "x_hi", "x_lo", "hid_ps", "hid", "y_ps", "out", "turn", "ids"]}

        def hold(eng, *waits):
            waits = [w for w in waits if w]
            for s, n in waits:
                eng.wait_ge(s, n)
            if any(not isinstance(n, int) for _, n in waits):
                one = spare[:, used_spare[0]:used_spare[0] + 1]
                used_spare[0] += 1
                if eng.engine == mybir.EngineType.Pool:
                    nc.gpsimd.tensor_tensor(one, half[0:1, 0:1], half[0:1, 0:1], ALU.add)
                else:
                    nc.vector.memset(one, 0.0)

        def plain(eng, wait):
            if wait:
                eng.wait_ge(*wait)

        def of(sem_, g, ago=0, per=1):
            n = (g.n - ago + 1) * per
            return None if isinstance(n, int) and n <= 0 else (sem_, n)

        def landed(sem_, g, per, ago=0):
            if isinstance(g.n, int):
                n = ((g.n - g.two) // 2 + 1 - ago // 2) * 16 * per
                return (sem_, n) if n > 0 else None
            return (sem_, (g.n + (2 - g.two - ago)) * (8 * per))

        block = ctx.enter_context(nc.Block())
        x_g = x.rearrange("(g t) n c -> g n t c", t=TPG)
        adj_g = adj.rearrange("(g t) n m -> g n t m", t=TPG)
        out_rows = out.rearrange("b n c -> (b n) c")
        N_LOADS = 14

        @block.sync
        def _(sp):
            sp.wait_ge(consts, 28)
            for dst, src in ((w_sb[:], g_w), (a12_sb[:], g_a12), (a_sb[:, 0:1], g_a1), (a_sb[:, 1:2], g_a2),
                             (w1g[:], g_w1), (w2v[:, 0:C], g_w2), (w1f[:], f_w1),
                             (b1f[:], f_b1.rearrange("(h p) -> p h", p=P)),
                             (wg[:, :, 0:NE], f_wg.rearrange("(h p) e -> p h e", p=P)),
                             (bg[0:1, :], f_bg.rearrange("(o e) -> o e", o=1))):
                sp.dma_start(dst, src, allow_slow_non_contiguous=True).then_inc(w_loaded, 16)
            for k in range(3):
                sp.dma_start(bd[k:k + 1, :], f_bd.rearrange("(o e) c -> o (e c)", o=1)).then_inc(bd_loaded, 16)

            def load(t):
                g = back(t, 0, NG)
                if g is None:
                    return
                after(sp, S["elu_pos"], g, RING)
                sp.dma_start(xb[:, g.ring], x_g[g.n] if isinstance(g.n, int) else
                             x_g[bass.ds(g.n, 1)].rearrange("o n t c -> (o n) t c")).then_inc(x_in[g.ring], 16)
                after(sp, S["mask_ok"], g, 2)
                sp.dma_start(adjb[:, g.two], adj_g[g.n] if isinstance(g.n, int) else
                             adj_g[bass.ds(g.n, 1)].rearrange("o n t c -> (o n) t c")).then_inc(adj_in[g.two], 16)
                if isinstance(g.n, int) and g.n == 1:
                    sp.dma_start(wd[:].rearrange("p (e h c) -> p e h c", e=NE, h=NCH),
                                 f_wd.rearrange("e (h p) c -> p e h c", p=P)).then_inc(wd_loaded, 16)

            slots(sp, load, NG, 0, PEEL1)

            for s in sent:
                sp.wait_ge(s, 16 * TPG * NG // 2)
            sp.wait_ge(pads_sent, 16 * NE)
            sp.wait_ge(pad0_sent, 16)
            sp.wait_ge(tab, 14)

            def load_rows(t):
                q = back(t, 0, NQ)
                if q is None:
                    return
                after(sp, C_["out"], q, RING)
                for b in range(TPG):
                    r = sp.value_load(row_tab[0:1, bass.ds(q.n * TPG + b, 1)], min_val=0, max_val=NE * REGION)
                    sp.dma_start(crow[:, q.ring, b, :], rows[bass.ds(r, P), :]).then_inc(rows_in[q.ring], 16)

            slots(sp, load_rows, NQ, 0, PEEL2)
            for i in range(2):
                sp.wait_ge(out_sent[i], 16 * TPG * NQ // 2)

        @block.gpsimd
        def _(pool):
            nc.gpsimd.memset(ident[:], 0.0).then_inc(consts, 1)
            nc.gpsimd.memset(before[:], 0.0).then_inc(consts, 1)
            nc.gpsimd.memset(ones_bf[:], 1.0).then_inc(consts, 1)
            nc.gpsimd.memset(ones_row[:], 1.0).then_inc(consts, 1)
            nc.gpsimd.memset(half[:], -0.5).then_inc(consts, 1)
            nc.gpsimd.memset(upto[:], 1.0).then_inc(consts, 1)
            nc.gpsimd.memset(padrow[:], 0.0).then_inc(consts, 1)
            nc.gpsimd.iota(first_i[:], pattern=[[-1, NE]], base=NE, channel_multiplier=0).then_inc(consts, 1)
            nc.gpsimd.iota(carry_i[:], pattern=[[REGION, NE]], base=0, channel_multiplier=0).then_inc(consts, 1)
            nc.gpsimd.iota(part_i[:], pattern=[[0, 1]], base=0, channel_multiplier=1).then_inc(consts, 1)
            nc.gpsimd.iota(tile_i[:], pattern=[[1, NT]], base=0, channel_multiplier=0).then_inc(consts, 1)
            nc.gpsimd.iota(tok_i[:], pattern=[[P, TPG]], base=0, channel_multiplier=1).then_inc(consts, 1)
            nc.gpsimd.memset(wg[:], 0.0).then_inc(consts, 1)
            nc.gpsimd.memset(pick[:], 0.0).then_inc(consts, 1)
            pool.wait_ge(consts, 14)
            nc.gpsimd.affine_select(out=ident[:], in_=ident[:], compare_op=ALU.not_equal, fill=1.0, base=0,
                                    pattern=[[-1, P]], channel_multiplier=1).then_inc(consts, 1)
            nc.gpsimd.affine_select(out=before[:], in_=before[:], compare_op=ALU.is_ge, fill=1.0, base=0,
                                    pattern=[[-1, P]], channel_multiplier=1).then_inc(consts, 1)
            nc.gpsimd.affine_select(out=upto[:], in_=upto[:], compare_op=ALU.is_ge, fill=0.0, base=0,
                                    pattern=[[1, NE], [-1, NE]], channel_multiplier=0).then_inc(consts, 1)
            for h in range(NCH):
                pool.wait_ge(consts, 17 + h)
                nc.gpsimd.affine_select(out=pick[:], in_=pick[:], compare_op=ALU.not_equal, fill=1.0,
                                        base=-QUAD * h, pattern=[[-1, NE]], channel_multiplier=1).then_inc(consts, 1)
            nc.gpsimd.iota(padrow[:, TOKEN:TOKEN + 1].bitcast(I32), pattern=[[0, 1]], base=TOKENS,
                           channel_multiplier=0).then_inc(consts, 1)
            nc.gpsimd.tensor_copy(first[:], first_i[:]).then_inc(consts, 1)
            nc.gpsimd.tensor_copy(carry[:], carry_i[:]).then_inc(consts, 1)
            nc.gpsimd.tensor_copy(region0[:], carry_i[:]).then_inc(consts, 1)
            nc.gpsimd.tensor_copy(part_f[:], part_i[:]).then_inc(consts, 1)
            nc.gpsimd.tensor_copy(tile_no[:], tile_i[:]).then_inc(consts, 1)
            nc.gpsimd.tensor_copy(tok[:], tok_i[:]).then_inc(consts, 1)
            pool.wait_ge(consts, 28)
            pool.dma_start(rows[NE * REGION:NE * REGION + P, :], padrow[:]).then_inc(pad0_sent, 16)

            def power(t, by, stats, var_eps, ve_, var_of, out_of, done, used):
                g = back(t, by, NG)
                if g is None:
                    return
                hold(pool, of(S[stats], g))
                nc.gpsimd.tensor_scalar(ve_[:, g.two], var_of(g), EPS, None, ALU.add).then_inc(S[var_eps], 1)
                hold(pool, of(S[var_eps], g), of(S[used], g, 2))
                nc.gpsimd.tensor_tensor(out_of(g), ve_[:, g.two], half[:], ALU.pow).then_inc(S[done], 1)

            def add(t):
                g = back(t, 4, NG)
                if g is None:
                    return
                after(pool, S["elu_pos"], g)
                after(pool, S["elu_neg"], g)
                plain(pool, landed(sent[g.two], g, TPG, RING))
                nc.gpsimd.tensor_tensor(rowb[:, g.ring, :, 0:C], ex[:, g.two], rr[:, g.two],
                                        ALU.add).then_inc(S["x2_ok"], 1)

            def number(t):
                g = back(t, 6, NG)
                if g is None:
                    return
                hold(pool, of(S["x2_ok"], g), of(S["tok_next"], g, 1))
                nc.gpsimd.tensor_copy(rowb[:, g.ring, :, TOKEN].bitcast(I32), tok[:]).then_inc(S["tok_ok"], 1)
                hold(pool, of(S["tok_ok"], g))
                nc.gpsimd.tensor_scalar(tok[:], tok[:], float(N), None, ALU.add).then_inc(S["tok_next"], 1)

            def send(t, tiles):
                g = back(t, 7, NG)
                if g is None:
                    return
                if tiles[0] == 0:
                    hold(pool, of(S["desti_ok"], g), of(S["prob_ok"], g), of(S["rstd2_ok"], g),
                         of(S["tok_ok"], g), landed(sent[g.two], g, TPG, 2))
                for b in tiles:
                    nc.gpsimd.indirect_dma_start(
                        rows[:, :], bass.IndirectOffsetOnAxis(desti[:, g.ring, b:b + 1], 0), rowb[:, g.ring, b, :], None,
                        bounds_check=NE * REGION - 1, oob_is_err=False).then_inc(sent[g.two], 16)

            def slot(t):
                send(t, (0, 1))
                add(t)
                send(t, (2, 3))
                power(t, 4, "stats2", "var_eps2", ve2, lambda g: rowb[:, g.ring, :, RSTD],
                      lambda g: rowb[:, g.ring, :, RSTD], "rstd2_ok", "xn_ok")
                power(t, 0, "stats", "var_eps", ve, lambda g: mv[:, g.two, :, 1],
                      lambda g: rstd[:, g.two], "rstd_ok", "fn_ok")
                number(t)

            slots(pool, slot, NG, DEPTH1, PEEL1)
            pool.wait_ge(pads_ready, 2)
            for e in range(NE):
                nc.gpsimd.indirect_dma_start(
                    rows[:, :], bass.IndirectOffsetOnAxis(padi[:, e:e + 1], 0), padrow[:], None,
                    bounds_check=NE * REGION - 1, oob_is_err=False).then_inc(pads_sent, 16)

            def send_out(t):
                q = back(t, 4, NQ)
                if q is None:
                    return
                plain(pool, of(C_["out"], q))
                plain(pool, of(C_["ids"], q))
                plain(pool, landed(out_sent[q.two], q, TPG, 2))
                nc.gpsimd.tensor_tensor(turn[:, q.ring:q.ring + 1], half[0:1, 0:1], half[0:1, 0:1],
                                        ALU.add).then_inc(C_["turn"], 1)
                for b in range(TPG):
                    nc.gpsimd.indirect_dma_start(
                        out_rows[:, :],
                        bass.IndirectOffsetOnAxis(ctok[:, q.ring, b:b + 1], 0),
                        cout[:, q.ring, b, :], None,
                        bounds_check=TOKENS - 1, oob_is_err=False).then_inc(out_sent[q.two], 16)

            slots(pool, send_out, NQ, DEPTH2, PEEL2)

        @block.tensor
        def _(pe):
            pe.wait_ge(consts, 28)
            pe.wait_ge(w_loaded, 16 * 10)
            nc.tensor.transpose(ps[:, 0, 0:P], w_sb[:], ident[:])
            nc.tensor.transpose(ps[:, 0, P:2 * P], a12_sb[:], ident[:]).then_inc(setup_pe, 1)
            pe.wait_ge(setup_dve, 2)
            nc.tensor.matmul(ps[:, 1, 0:C], a12T[:], wT[:], start=True, stop=True)
            nc.tensor.matmul(ps[:, 1, 256:258], wT[:], a_sb[:], start=True, stop=True)
            nc.tensor.matmul(ps[:, 1, 320:320 + NE], ones_row[:], bg[0:1, :], start=True, stop=True).then_inc(setup_pe, 1)
            pe.wait_ge(setup_dve, 6)
            nc.tensor.matmul(ps[:, 2, 0:C], wT[:], a12wT[:], start=True, stop=True).then_inc(setup_pe, 1)
            pe.wait_ge(setup_dve, 7)

            def t_fT(t):
                g = back(t, 1, NG)
                if g is None:
                    return
                after(pe, S["fn_ok"], g)
                after(pe, S["leaky_ok"], g, 2)
                for b in range(TPG):
                    m = nc.tensor.transpose(bank(B_L)[:, b, :], fn[:, g.two, b, :], ident[:])
                m.then_inc(S["fT_ps"], 1)

            def t_g(t):
                g = back(t, 1, NG)
                if g is None:
                    return
                after(pe, S["fT_ok"], g)
                after(pe, S["gT_ok"], g, 1)
                after(pe, S["gS_ok"], g, 5)
                nc.tensor.matmul(ps[:, B_G, :], pair[:], fT[:, g.ring], start=True, stop=True).then_inc(S["g_ps"], 1)

            def t_f2(t):
                g = back(t, 2, NG)
                if g is None:
                    return
                after(pe, S["f2_ok"], g, 1)
                after(pe, S["pos_ok"], g, 5)
                after(pe, S["carried"], g, 5)
                for b in range(TPG):
                    m = nc.tensor.matmul(ps_f2[:, b, :] if b < F2_IN else ps_f2b[:, 0, :],
                                         fT[:, g.ring, b * P:(b + 1) * P], w2v[:], start=True, stop=True)
                m.then_inc(S["f2_ps"], 1)

            def t_lg(t):
                g = back(t, 2, NG)
                if g is None:
                    return
                after(pe, S["gT_ok"], g)
                after(pe, S["fT_ok"], g, -1, last=NG)
                after(pe, S["leaky_ok"], g, 1)
                for b in range(TPG):
                    m = nc.tensor.matmul(bank(B_L)[:, b, :], gT[:, g.two, b * P:(b + 1) * P],
                                         fT[:, g.ring, b * P:(b + 1) * P], start=True, stop=True)
                m.then_inc(S["lg_ps"], 1)

            def t_pT(t):
                g = back(t, 3, NG)
                if g is None:
                    return
                after(pe, S["probs_n"], g)
                after(pe, S["xT_ok"], g, 2)
                for b in range(TPG):
                    m = nc.tensor.transpose(bank(B_TR)[:, b, :], pr[:, g.two, b, :], ident[:])
                m.then_inc(S["pT_ps"], 1)

            def t_hout(t):
                g = back(t, 3, NG)
                if g is None:
                    return
                after(pe, S["pT_ok"], g)
                after(pe, S["f2_ok"], g)
                after(pe, S["elu_pos"], g, 1)
                after(pe, S["expm"], g, 1)
                for b in range(TPG):
                    nc.tensor.matmul(bank(B_H)[:, b, :], fT[:, g.ring, b * P:(b + 1) * P], w1g[:], start=True, stop=False)
                    m = nc.tensor.matmul(bank(B_H)[:, b, :], pT[:, g.two, b * P:(b + 1) * P], f2[:, g.ring, b, :],
                                         start=False, stop=True)
                m.then_inc(S["hout_ps"], 1)

            def t_xT(t):
                g = back(t, 5, NG)
                if g is None:
                    return
                after(pe, S["xn_ok"], g)
                after(pe, S["pT_ok"], g, -1, last=NG)
                for b in range(TPG):
                    m = nc.tensor.transpose(bank(B_TR)[:, b, :], xn2[:, g.two, b, :], ident[:])
                m.then_inc(S["xT_ps"], 1)

            def t_hid(t, chunks):
                g = back(t, 5, NG)
                if g is None:
                    return
                after(pe, S["xT_ok"], g)
                for h in chunks:
                    n = g.n * NCH + h - 1
                    if not (isinstance(n, int) and n <= 0):
                        pe.wait_ge(S["hid_ok"], n)
                    nc.tensor.matmul(ps[:, B_HID + h % 2, :], w1f[:, h * P:(h + 1) * P], xT[:, g.two],
                                     start=True, stop=True).then_inc(S["hid_ps"], 1)

            def t_gcol(t):
                g = back(t, 6, NG)
                if g is None:
                    return
                after(pe, S["hid_ok"], g, 0, NCH)
                after(pe, S["gT_ok"], g, -4, last=NG)
                after(pe, S["gS_ok"], g, 1)
                for h in range(NCH):
                    m = nc.tensor.matmul(ps[QUAD * h:QUAD * (h + 1), B_G, :], wg[:, h, :], hT[:, g.two, h, :],
                                         start=True, stop=True)
                m.then_inc(S["gcol_ps"], 1)

            def t_gate(t):
                g = back(t, 6, NG)
                if g is None:
                    return
                after(pe, S["gS_ok"], g)
                after(pe, S["pos_ok"], g, 1)
                after(pe, S["carried"], g, 1)
                after(pe, S["f2_ok"], g, -4, last=NG)
                for b in range(TPG):
                    m = nc.tensor.matmul(ps_gate[:, b, :], gS[:, g.two, b * P:(b + 1) * P], pick[:],
                                         start=True, stop=True)
                m.then_inc(S["gate_ps"], 1)

            def t_rank(t):
                g = back(t, 6, NG)
                if g is None:
                    return
                after(pe, S["hot_ok"], g)
                for b in range(TPG):
                    nc.tensor.matmul(ps_rank[:, b, :], before[:], hot[:, g.two, b, :], start=True, stop=(b == 0))
                    for a in range(b):
                        nc.tensor.matmul(ps_rank[:, b, :], ones_bf[:], hot[:, g.two, a, :], start=False,
                                         stop=(a == b - 1))
                for b in range(TPG):
                    m = nc.tensor.matmul(ps_tot, ones_bf[:], hot[:, g.two, b, :], start=(b == 0), stop=(b == TPG - 1))
                m.then_inc(S["rank_ps"], 1)

            def slot(t):
                t_gcol(t)
                t_xT(t)
                t_fT(t)
                t_f2(t)
                t_lg(t)
                t_pT(t)
                t_gate(t)
                t_hid(t, (0, 1))
                t_g(t)
                t_hid(t, (2, 3))
                t_hout(t)
                t_rank(t)

            slots(pe, slot, NG, DEPTH1, PEEL1)

            pe.wait_ge(tab, 14)
            pe.wait_ge(wd_loaded, 16)
            pe.wait_ge(parts, 9)

            def c_xT(t):
                q = back(t, 1, NQ)
                if q is None:
                    return
                after(pe, C_["xn"], q)
                after(pe, C_["x_lo"], q, 1)
                for b in range(TPG):
                    m = nc.tensor.transpose(bank(B_TR)[:, b, :], cxn[:, q.two, b, :], ident[:])
                m.then_inc(C_["xT_ps"], 1)

            def c_hid(t, h):
                q = back(t, 2, NQ)
                if q is None:
                    return
                after(pe, C_["x_hi"], q)
                after(pe, C_["x_lo"], q)
                n = q.n * NCH + h - 1
                if not (isinstance(n, int) and n <= 0):
                    pe.wait_ge(C_["hid"], n)
                w_hi, w_lo = w1_hi[:, h * P:(h + 1) * P], w1_lo[:, h * P:(h + 1) * P]
                nc.tensor.matmul(ps[:, B_HID + h % 2, :], w_hi, cx_hi[:, q.two], start=True, stop=False)
                nc.tensor.matmul(ps[:, B_HID + h % 2, :], w_lo, cx_hi[:, q.two], start=False, stop=False)
                nc.tensor.matmul(ps[:, B_HID + h % 2, :], w_hi, cx_lo[:, q.two], start=False,
                                 stop=True).then_inc(C_["hid_ps"], 1)

            def c_experts(t):
                q = back(t, 3, NQ)
                if q is None:
                    return
                return nc.values_load_multi_w_load_instructions(
                    wd_tab[0:1, bass.ds(q.n * TPG, TPG)], [mybir.EngineType.PE], min_val=0, max_val=NE - 1)[1]

            def c_y(t, experts, b):
                q = back(t, 3, NQ)
                if q is None:
                    return
                w = experts[b]
                after(pe, C_["hid"], q, 0, NCH)
                after(pe, C_["out"], q, 2)
                nc.tensor.matmul(bank(B_Y + q.two)[:, b, :], ones_bf[0:3, :], bd3[:, bass.ds(w * C, C)],
                                 start=True, stop=False)
                for h in range(NCH):
                    m = nc.tensor.matmul(bank(B_Y + q.two)[:, b, :], chT[:, q.two, h, b * P:(b + 1) * P],
                                         wd[:, bass.ds(w * (NCH * C) + h * C, C)], start=False,
                                         stop=(h == NCH - 1))
                m.then_inc(C_["y_ps"], 1)

            def slot_c(t):
                experts = c_experts(t)
                c_hid(t, 0)
                c_y(t, experts, 0)
                c_hid(t, 1)
                c_y(t, experts, 1)
                c_xT(t)
                c_hid(t, 2)
                c_y(t, experts, 2)
                c_hid(t, 3)
                c_y(t, experts, 3)

            slots(pe, slot_c, NQ, DEPTH2, PEEL2)

        @block.scalar
        def _(act):
            act.wait_ge(setup_dve, 7)

            def a_fT(t):
                g = back(t, 1, NG)
                if g is None:
                    return
                after(act, S["fT_ps"], g)
                after(act, S["hout_ps"], g, RING)
                nc.scalar.copy(fT[:, g.ring], ps[:, B_L, :]).then_inc(S["fT_ok"], 1)

            def a_gT(t):
                g = back(t, 1, NG)
                if g is None:
                    return
                after(act, S["g_ps"], g)
                after(act, S["lg_ps"], g, 2)
                nc.scalar.activation(gT[:, g.two], ps[:, B_G, :], ACT.Identity, bias=uv[:, 0:1]).then_inc(S["gT_ok"], 1)

            def a_mask(t):
                g = back(t, 1, NG)
                if g is None:
                    return
                plain(act, landed(adj_in[g.two], g, 1))
                after(act, S["masked"], g, 2)
                nc.scalar.activation(maskb[:, g.two], adjb[:, g.two], ACT.Copy, bias=-OPEN,
                                     scale=2.0 * OPEN).then_inc(S["mask_ok"], 1)

            def a_pT(t):
                g = back(t, 3, NG)
                if g is None:
                    return
                after(act, S["pT_ps"], g)
                after(act, S["hout_ps"], g, 2)
                nc.scalar.copy(pT[:, g.two], ps[:, B_TR, :]).then_inc(S["pT_ok"], 1)

            def a_gS(t):
                g = back(t, 6, NG)
                if g is None:
                    return
                after(act, S["gcol_ps"], g)
                after(act, S["gate_ps"], g, 2)
                nc.scalar.copy(gS[:, g.two], ps[:, B_G, :]).then_inc(S["gS_ok"], 1)

            def a_relu(t):
                g = back(t, 2, NG)
                if g is None:
                    return
                after(act, S["lg_ps"], g)
                after(act, S["vcol_ok"], g)
                after(act, S["leaky_ok"], g, 2)
                for b in range(TPG):
                    m = nc.scalar.activation(relu[:, g.two, b, :], bank(B_L)[:, b, :], ACT.Relu,
                                             bias=vcol[:, g.two, b:b + 1], scale=1.0 - SLOPE)
                m.then_inc(S["relu_ok"], 1)

            def a_exp(t):
                g = back(t, 3, NG)
                if g is None:
                    return
                after(act, S["nmax_ok"], g)
                after(act, S["pT_ps"], g, 2)
                after(act, S["rsum_ok"], g, 2)
                for b in range(TPG):
                    nc.scalar.activation(pr[:, g.two, b, :], lg[:, g.two, b, :], ACT.Exp, bias=nmax[:, g.two, b:b + 1],
                                         accum_out=psumr[:, g.two, b:b + 1]).then_inc(S["probs"], 1)

            def a_expm(t):
                g = back(t, 4, NG)
                if g is None:
                    return
                after(act, S["hout_ps"], g)
                after(act, S["x2_ok"], g, 2)
                nc.scalar.activation(ex[:, g.two], bank(B_H), ACT.Exp).then_inc(S["expm"], 1)

            def a_xT(t):
                g = back(t, 5, NG)
                if g is None:
                    return
                after(act, S["xT_ps"], g)
                after(act, S["hid_ps"], g, 2, NCH)
                nc.scalar.copy(xT[:, g.two], ps[:, B_TR, :]).then_inc(S["xT_ok"], 1)

            def a_gelu(t, chunks):
                g = back(t, 5, NG)
                if g is None:
                    return
                after(act, S["gcol_ps"], g, 2)
                for h in chunks:
                    act.wait_ge(S["hid_ps"], g.n * NCH + (h + 1))
                    nc.scalar.activation(hT[:, g.two, h, :], ps[:, B_HID + h % 2, :], ACT.Gelu,
                                         bias=b1f[:, h:h + 1]).then_inc(S["hid_ok"], 1)

            def a_gate(t):
                g = back(t, 7, NG)
                if g is None:
                    return
                after(act, S["gd_ok"], g)
                after(act, S["gs_ok"], g, 2)
                nc.scalar.activation(ge[:, g.two], gd[:, g.two], ACT.Exp).then_inc(S["gate_exp"], 1)

            def slot(t):
                a_gate(t)
                a_expm(t)
                a_exp(t)
                a_fT(t)
                a_gS(t)
                a_xT(t)
                a_relu(t)
                a_pT(t)
                a_gelu(t, (0, 1))
                a_gT(t)
                a_gelu(t, (2,))
                a_mask(t)
                a_gelu(t, (3,))

            slots(act, slot, NG, DEPTH1, PEEL1)

            def c_hi(t):
                q = back(t, 1, NQ)
                if q is None:
                    return
                after(act, C_["xT_ps"], q)
                after(act, C_["x_lo"], q, 2)
                after(act, C_["hid_ps"], q, 2, NCH)
                nc.scalar.copy(cx_hi[:, q.two], ps[:, B_TR, :]).then_inc(C_["x_hi"], 1)

            def c_gelu(t, chunks):
                q = back(t, 2, NQ)
                if q is None:
                    return
                after(act, C_["y_ps"], q, 2, TPG)
                for h in chunks:
                    act.wait_ge(C_["hid_ps"], q.n * NCH + (h + 1))
                    nc.scalar.activation(chT[:, q.two, h, :], ps[:, B_HID + h % 2, :], ACT.Gelu,
                                         bias=b1f[:, h:h + 1]).then_inc(C_["hid"], 1)

            def slot_c(t):
                c_gelu(t, (0, 1))
                c_hi(t)
                c_gelu(t, (2, 3))

            slots(act, slot_c, NQ, DEPTH2, PEEL2)

        @block.vector
        def _(dve):
            V = nc.vector
            dve.wait_ge(consts, 28)
            dve.wait_ge(bd_loaded, 16 * 3)
            V.tensor_copy(bd_hi[:], bd[:]).then_inc(parts, 1)
            dve.wait_ge(parts, 1)
            V.tensor_tensor(bd_rest[:], bd[:], bd_hi[:], ALU.subtract).then_inc(parts, 1)
            V.tensor_scalar(bd_some[:], bd_hi[:], ident[0:3, 0:1], None, ALU.mult).then_inc(parts, 1)
            dve.wait_ge(parts, 2)
            V.tensor_copy(bd_mid[:], bd_rest[:]).then_inc(parts, 1)
            dve.wait_ge(parts, 4)
            V.tensor_tensor(bd_low[:], bd_rest[:], bd_mid[:], ALU.subtract).then_inc(parts, 1)
            V.scalar_tensor_tensor(bd_some[:], bd_mid[:], ident[0:3, 1:2], bd_some[:], ALU.mult,
                                   ALU.add).then_inc(parts, 1)
            dve.wait_ge(parts, 6)
            V.scalar_tensor_tensor(bd3[:], bd_low[:], ident[0:3, 2:3], bd_some[:], ALU.mult,
                                   ALU.add).then_inc(parts, 1)
            dve.wait_ge(w_loaded, 16 * 10)
            V.tensor_copy(w1_hi[:], w1f[:]).then_inc(parts, 1)
            dve.wait_ge(parts, 8)
            V.tensor_tensor(w1_lo[:], w1f[:], w1_hi[:].bitcast(F32), ALU.subtract).then_inc(parts, 1)
            dve.wait_ge(setup_pe, 1)
            V.tensor_copy(wT[:], ps[:, 0, 0:P]).then_inc(setup_dve, 1)
            V.tensor_copy(a12T[:], ps[:, 0, P:2 * P]).then_inc(setup_dve, 1)
            dve.wait_ge(setup_pe, 2)
            V.tensor_copy(a12wT[:], ps[:, 1, 0:C]).then_inc(setup_dve, 1)
            V.tensor_copy(uv[:], ps[:, 1, 256:258]).then_inc(setup_dve, 1)
            V.tensor_copy(w2v[:, C:C + 1], ps[:, 1, 257:258]).then_inc(setup_dve, 1)
            V.tensor_copy(bg[:], ps[:, 1, 320:320 + NE]).then_inc(setup_dve, 1)
            dve.wait_ge(setup_pe, 3)
            V.tensor_copy(pair[:], ps[:, 2, 0:C]).then_inc(setup_dve, 1)
            dve.wait_ge(consts, 28)
            dve.wait_ge(setup_dve, 7)

            def x_ready(g):
                if isinstance(g.n, int):
                    dve.wait_ge(x_in[g.ring], 16 * (g.n // RING + 1))
                else:
                    dve.wait_ge(x_in[g.ring], (g.n + (RING - g.ring)) * (16 // RING))

            def d_stats(t):
                g = back(t, 0, NG)
                if g is None:
                    return
                x_ready(g)
                after(dve, S["var_eps"], g, 2)
                for b in range(TPG):
                    m = V.bn_stats(bn[:, g.two, b, :], xb[:, g.ring, b, :])
                m.then_inc(S["bn_ok"], 1)

            def d_aggr(t):
                g = back(t, 0, NG)
                if g is None:
                    return
                hold(dve, of(S["bn_ok"], g))
                for b in range(TPG):
                    m = V.bn_aggr(mv[:, g.two, b, :], bn[:, g.two, b, :])
                m.then_inc(S["stats"], 1)

            def d_norm(t):
                g = back(t, 1, NG)
                if g is None:
                    return
                after(dve, S["rstd_ok"], g)
                after(dve, S["fT_ps"], g, 2)
                for b in range(TPG):
                    m = V.tensor_scalar(fn[:, g.two, b, :], xb[:, g.ring, b, :], mv[:, g.two, b, 0:1],
                                        rstd[:, g.two, b:b + 1], ALU.subtract, ALU.mult)
                m.then_inc(S["fn_ok"], 1)

            def d_v(t):
                g = back(t, 2, NG)
                if g is None:
                    return
                after(dve, S["f2_ps"], g)
                after(dve, S["relu_ok"], g, 2)
                V.tensor_scalar(vcol[:, g.two, 0:F2_IN], ps_f2[:, :, C], 1.0 - SLOPE, None, ALU.mult)
                V.tensor_scalar(vcol[:, g.two, F2_IN:TPG], ps_f2b[:, :, C], 1.0 - SLOPE, None,
                                ALU.mult).then_inc(S["vcol_ok"], 1)

            def d_f2(t):
                g = back(t, 2, NG)
                if g is None:
                    return
                after(dve, S["f2_ps"], g)
                after(dve, S["hout_ps"], g, RING)
                V.tensor_copy(f2[:, g.ring, 0:F2_IN], ps_f2[:, :, 0:C])
                V.tensor_copy(f2[:, g.ring, F2_IN:TPG], ps_f2b[:, :, 0:C]).then_inc(S["f2_ok"], 1)

            def d_leaky(t):
                g = back(t, 2, NG)
                if g is None:
                    return
                after(dve, S["relu_ok"], g)
                after(dve, S["probs"], g, 2, TPG)
                V.scalar_tensor_tensor(lg[:, g.two], bank(B_L), SLOPE, relu[:, g.two], ALU.mult,
                                       ALU.add).then_inc(S["leaky_ok"], 1)

            def d_mask(t):
                g = back(t, 2, NG)
                if g is None:
                    return
                after(dve, S["leaky_ok"], g)
                after(dve, S["mask_ok"], g)
                V.scalar_tensor_tensor(lg[:, g.two], maskb[:, g.two], NEG, lg[:, g.two], ALU.max,
                                       ALU.min).then_inc(S["masked"], 1)

            def d_max(t):
                g = back(t, 2, NG)
                if g is None:
                    return
                after(dve, S["masked"], g)
                after(dve, S["probs"], g, 2, TPG)
                V.tensor_reduce(nmax[:, g.two], lg[:, g.two], AX.X, ALU.max, negate=True).then_inc(S["nmax_ok"], 1)

            def d_probs(t):
                g = back(t, 3, NG)
                if g is None:
                    return
                after(dve, S["probs"], g, 0, TPG)
                V.reciprocal(rsum[:, g.two], psumr[:, g.two]).then_inc(S["rsum_ok"], 1)

            def d_probs_n(t):
                g = back(t, 3, NG)
                if g is None:
                    return
                after(dve, S["rsum_ok"], g)
                V.tensor_tensor(pr[:, g.two], pr[:, g.two], rsum[:, g.two].unsqueeze(2).to_broadcast([P, TPG, P]),
                                ALU.mult).then_inc(S["probs_n"], 1)

            def d_elu(t):
                g = back(t, 4, NG)
                if g is None:
                    return
                after(dve, S["hout_ps"], g)
                after(dve, S["x2_ok"], g, 2)
                after(dve, S["expm"], g)
                V.scalar_tensor_tensor(rr[:, g.two], bank(B_H), 0.0, xb[:, g.ring], ALU.max,
                                       ALU.add).then_inc(S["elu_pos"], 1)
                V.tensor_scalar(ex[:, g.two], ex[:, g.two], 1.0, -1.0, ALU.min, ALU.add).then_inc(S["elu_neg"], 1)

            def d_stats2(t):
                g = back(t, 4, NG)
                if g is None:
                    return
                after(dve, S["x2_ok"], g)
                for b in range(TPG):
                    m = V.bn_stats(bn2[:, g.two, b, :], rowb[:, g.ring, b, 0:C])
                m.then_inc(S["bn2_ok"], 1)

            def d_aggr2(t):
                g = back(t, 4, NG)
                if g is None:
                    return
                hold(dve, of(S["bn2_ok"], g), of(S["var_eps2"], g, 2))
                for b in range(TPG):
                    m = V.bn_aggr(rowb[:, g.ring, b, MEAN:MEAN + 2], bn2[:, g.two, b, :])
                m.then_inc(S["stats2"], 1)

            def d_norm2(t):
                g = back(t, 5, NG)
                if g is None:
                    return
                after(dve, S["rstd2_ok"], g)
                after(dve, S["xT_ps"], g, 2)
                for b in range(TPG):
                    m = V.tensor_scalar(xn2[:, g.two, b, :], rowb[:, g.ring, b, 0:C], rowb[:, g.ring, b, MEAN:MEAN + 1],
                                        rowb[:, g.ring, b, RSTD:RSTD + 1], ALU.subtract, ALU.mult)
                m.then_inc(S["xn_ok"], 1)

            def wide(v):
                return v.unsqueeze(2).to_broadcast([P, TPG, NE])

            def d_gate(t, k):
                g = back(t, 6, NG)
                if g is None:
                    return
                if k == 0:
                    after(dve, S["gate_ps"], g)
                    V.tensor_tensor(gl[:, g.two], ps_gate, bg[:].unsqueeze(1).to_broadcast([P, TPG, NE]),
                                    ALU.add).then_inc(S["gl_ok"], 1)
                if k == 1:
                    after(dve, S["gl_ok"], g)
                    V.tensor_reduce(gmx[:, g.two], gl[:, g.two], AX.X, ALU.max).then_inc(S["gmx_ok"], 1)
                if k == 2:
                    after(dve, S["gmx_ok"], g)
                    after(dve, S["gate_exp"], g, 2)
                    V.tensor_tensor(gd[:, g.two], gl[:, g.two], wide(gmx[:, g.two]), ALU.subtract).then_inc(S["gd_ok"], 1)
                    V.tensor_tensor(hit[:, g.two], gl[:, g.two], wide(gmx[:, g.two]), ALU.is_equal).then_inc(S["hit0"], 1)
                if k == 3:
                    after(dve, S["hit0"], g)
                    V.tensor_tensor(hit[:, g.two], hit[:, g.two], first[:].unsqueeze(1).to_broadcast([P, TPG, NE]),
                                    ALU.mult).then_inc(S["hit1"], 1)
                if k == 4:
                    after(dve, S["hit1"], g)
                    V.tensor_reduce(hmx[:, g.two], hit[:, g.two], AX.X, ALU.max).then_inc(S["hmx_ok"], 1)
                if k == 5:
                    after(dve, S["hmx_ok"], g)
                    after(dve, S["rank_ps"], g, 2)
                    V.tensor_tensor(hot[:, g.two], hit[:, g.two], wide(hmx[:, g.two]),
                                    ALU.is_equal).then_inc(S["hot_ok"], 1)

            def d_prob(t, k):
                g = back(t, 7, NG)
                if g is None:
                    return
                if k == 0:
                    after(dve, S["gate_exp"], g)
                    V.tensor_reduce(gs[:, g.two], ge[:, g.two], AX.X, ALU.add).then_inc(S["gs_ok"], 1)
                if k == 1:
                    after(dve, S["gs_ok"], g)
                    V.reciprocal(rowb[:, g.ring, :, PROB], gs[:, g.two]).then_inc(S["prob_ok"], 1)

            def d_route(t, k):
                g = back(t, 7, NG)
                if g is None:
                    return
                if k == 0:
                    after(dve, S["rank_ps"], g)
                    after(dve, S["carried"], g, 1)
                    V.tensor_tensor(pos[:, g.two], ps_rank, carry[:].unsqueeze(1).to_broadcast([P, TPG, NE]),
                                    ALU.add).then_inc(S["pos_ok"], 1)
                if k == 1:
                    after(dve, S["pos_ok"], g)
                    V.tensor_tensor(carry[:], ps_tot, carry[:], ALU.add).then_inc(S["carried"], 1)
                    V.tensor_tensor(pos2[:, g.two], pos[:, g.two], hot[:, g.two], ALU.mult).then_inc(S["pos_hot"], 1)
                if k == 2:
                    after(dve, S["pos_hot"], g)
                    V.tensor_reduce(dest[:, g.two], pos2[:, g.two], AX.X, ALU.add).then_inc(S["dest_ok"], 1)
                if k == 3:
                    after(dve, S["dest_ok"], g)
                    V.tensor_copy(desti[:, g.ring], dest[:, g.two]).then_inc(S["desti_ok"], 1)

            def slot(t):
                d_norm2(t)
                d_route(t, 0)
                d_prob(t, 0)
                d_route(t, 1)
                d_norm(t)
                d_route(t, 2)
                d_prob(t, 1)
                d_route(t, 3)
                d_elu(t)
                d_v(t)
                d_probs(t)
                d_probs_n(t)
                d_f2(t)
                d_stats2(t)
                d_leaky(t)
                d_aggr2(t)
                d_stats(t)
                d_mask(t)
                d_aggr(t)
                d_gate(t, 0)
                d_gate(t, 1)
                d_max(t)
                d_gate(t, 2)
                d_gate(t, 3)
                d_gate(t, 4)
                d_gate(t, 5)

            slots(dve, slot, NG, DEPTH1, PEEL1)

            done = [0]

            def step(ins):
                done[0] += 1
                ins.then_inc(tab, 1)
                dve.wait_ge(tab, done[0])

            dve.wait_ge(S["carried"], NG)
            V.tensor_scalar(padf[:], carry[:], part_f[:, 0:1], None, ALU.add).then_inc(pads_ready, 1)
            dve.wait_ge(pads_ready, 1)
            V.tensor_copy(padi[:], padf[:]).then_inc(pads_ready, 1)
            step(V.tensor_tensor(cnt[:], carry[:], region0[:], ALU.subtract))
            step(V.tensor_scalar(cnti[:], cnt[:], float(P - 1), None, ALU.add))
            step(V.tensor_scalar(cntj[:], cnti[:], 7, None, ALU.arith_shift_right))
            step(V.tensor_copy(ntile[:], cntj[:]))
            step(V.tensor_tensor(upn[:], upto[:], ntile[:].unsqueeze(1).to_broadcast([P, NE, NE]), ALU.mult))
            step(V.tensor_reduce(incl[:], upn[:], AX.X, ALU.add))
            step(V.tensor_tensor(past[:], tile_no[:].unsqueeze(2).to_broadcast([P, NT, NE]),
                                 incl[:].unsqueeze(1).to_broadcast([P, NT, NE]), ALU.is_ge))
            step(V.tensor_reduce(tex[:], past[:], AX.X, ALU.add))
            step(V.tensor_tensor(past2[:], past[:], ntile[:].unsqueeze(1).to_broadcast([P, NT, NE]), ALU.mult))
            step(V.tensor_reduce(tst[:], past2[:], AX.X, ALU.add))
            step(V.tensor_tensor(trow[:], tile_no[:], tst[:], ALU.subtract))
            step(V.scalar_tensor_tensor(trow2[:], tex[:], float(REGION // P), trow[:], ALU.mult, ALU.add))
            step(V.tensor_scalar(row_tab[:], trow2[:], float(P), float(NE * REGION), ALU.mult, ALU.min))
            step(V.tensor_scalar(wd_tab[:], tex[:], float(NE - 1), None, ALU.min))

            def c_norm(t):
                q = back(t, 1, NQ)
                if q is None:
                    return
                if isinstance(q.n, int):
                    dve.wait_ge(rows_in[q.ring], 16 * TPG * (q.n // RING + 1))
                else:
                    dve.wait_ge(rows_in[q.ring], (q.n + (RING - q.ring)) * (16 * TPG // RING))
                after(dve, C_["xT_ps"], q, 2)
                for b in range(TPG):
                    m = V.tensor_scalar(cxn[:, q.two, b, :], crow[:, q.ring, b, 0:C], crow[:, q.ring, b, MEAN:MEAN + 1],
                                        crow[:, q.ring, b, RSTD:RSTD + 1], ALU.subtract, ALU.mult)
                m.then_inc(C_["xn"], 1)

            def c_lo(t):
                q = back(t, 1, NQ)
                if q is None:
                    return
                after(dve, C_["xT_ps"], q)
                after(dve, C_["x_hi"], q)
                after(dve, C_["hid_ps"], q, 2, NCH)
                V.tensor_tensor(cx_lo[:, q.two], ps[:, B_TR, :], cx_hi[:, q.two].bitcast(F32),
                                ALU.subtract).then_inc(C_["x_lo"], 1)

            def c_out(t):
                q = back(t, 3, NQ)
                if q is None:
                    return
                plain(dve, landed(out_sent[q.two], q, TPG, RING))
                plain(dve, of(C_["turn"], q, RING))
                V.tensor_copy(ctok[:, q.ring], crow[:, q.ring, :, TOKEN].bitcast(I32)).then_inc(C_["ids"], 1)
                after(dve, C_["y_ps"], q, 0, TPG)
                for b in range(TPG):
                    m = V.scalar_tensor_tensor(cout[:, q.ring, b, :], bank(B_Y + q.two)[:, b, :],
                                               crow[:, q.ring, b, PROB:PROB + 1], crow[:, q.ring, b, 0:C],
                                               ALU.mult, ALU.add)
                m.then_inc(C_["out"], 1)

            def slot_c(t):
                c_norm(t)
                c_lo(t)
                c_out(t)

            slots(dve, slot_c, NQ, DEPTH2, PEEL2)


INPUTS = ["x", "adj", "L0_gnn_W", "L0_gnn_a_1", "L0_gnn_a_2", "L0_gnn_a_12", "L0_gnn_W_1", "L0_gnn_W_2",
          "L0_ffn_W1", "L0_ffn_b1", "L0_ffn_Wg", "L0_ffn_bg", "L0_ffn_Wd", "L0_ffn_bd"]


def kernel(**inputs):
    import numpy as np
    import concourse.bacc as bacc
    from concourse.bass_utils import run_bass_kernel_spmd

    nc = bacc.Bacc("TRN2", target_bir_lowering=False, num_devices=1)
    arrays, args = {}, []
    for name in INPUTS:
        a = np.ascontiguousarray(inputs[name])
        arrays[name] = a
        args.append(nc.dram_tensor(name, a.shape, mybir.dt.from_np(a.dtype), kind="ExternalInput").ap())
    nb, n, _ = inputs["x"].shape
    ne = inputs["L0_ffn_Wd"].shape[0]
    rows = nc.dram_tensor("rows", (ne * (nb * n + P) + P, ROW), F32).ap()
    out = nc.dram_tensor("out", inputs["x"].shape, F32, kind="ExternalOutput").ap()
    build(nc, *args, rows, out)
    return run_bass_kernel_spmd(nc, [arrays], core_ids=[0]).results[0]["out"]
```

```python
from contextlib import ExitStack

import concourse.bass as bass
from concourse import mybir

F32 = mybir.dt.float32
I32 = mybir.dt.int32
BF16 = mybir.dt.bfloat16
F32R = mybir.dt.float32r
ALU = mybir.AluOpType
ACT = mybir.ActivationFunctionType
AX = mybir.AxisListType

QUAD = 32
P = 128
TPG = 4
RING = 4
SLOPE = 0.2
NEG = -9.0e15
EPS = 1e-5
ROW = 132
PROB, TOKEN, MEAN, RSTD = 128, 129, 130, 131


class Group:

    def __init__(self, n, ring):
        self.n, self.ring = n, ring % RING
        self.two = self.ring % 2


def slots(eng, emit, n_groups, depth, peeled):
    looped = (n_groups - peeled) // RING * RING
    for t in range(peeled):
        emit(Group(t, t))
    with eng.Fori(peeled // RING, (peeled + looped) // RING) as k:
        for j in range(RING):
            emit(Group(k * RING + j, j))
    for t in range(peeled + looped, n_groups + depth):
        emit(Group(t, t))


def back(t, by, n_groups):
    n = t.n - by
    if isinstance(n, int) and not 0 <= n < n_groups:
        return None
    return Group(n, t.ring - by)


def after(eng, sem, g, ago=0, per=1, last=None):
    n = (g.n - ago + 1) * per
    if isinstance(n, int):
        if n <= 0:
            return
        if last is not None:
            n = min(n, last * per)
    eng.wait_ge(sem, n)


def build(nc, x, adj, g_w, g_a1, g_a2, g_a12, g_w1, g_w2, f_w1, f_b1, f_wg, f_bg, f_wd, f_bd, rows, out):
    NB = x.shape[0]
    C = x.shape[2]
    HID = f_w1.shape[1]
    NE = f_wd.shape[0]
    NCH = HID // P
    NG = NB // TPG
    N = TPG * P
    TOKENS = NB * P
    REGION = TOKENS + P
    NT = TOKENS // P + NE
    NQ = NT // TPG
    DEPTH1, PEEL1 = 7, 12
    DEPTH2, PEEL2 = 4, 8

    ctx = ExitStack()
    with ctx:
        def sb(name, shape, dt=F32):
            return ctx.enter_context(nc.sbuf_tensor(name, shape, dt))

        def sem(name):
            return ctx.enter_context(nc.semaphore(name))

        w_sb, a12_sb = sb("w_sb", [P, C]), sb("a12_sb", [P, C])
        a_sb = sb("a_sb", [P, 2])
        wT, a12T, a12wT = sb("wT", [P, C]), sb("a12T", [P, C]), sb("a12wT", [P, C])
        pair = sb("pair", [P, C])
        uv = sb("uv", [P, 2])
        w1g = sb("w1g", [P, C])
        w2v = sb("w2v", [P, C + 1])
        w1f = sb("w1f", [P, HID])
        w1_hi, w1_lo = sb("w1_hi", [P, HID], F32R), sb("w1_lo", [P, HID], F32R)
        b1f = sb("b1f", [P, NCH])
        wg = sb("wg", [P, NCH, QUAD])
        bg = sb("bg", [P, NE])
        wd = sb("wd", [P, NE * NCH * C])
        bd = sb("bd", [3, NE * C])
        bd_rest = sb("bd_rest", [3, NE * C])
        bd_hi, bd_mid = sb("bd_hi", [3, NE * C], BF16), sb("bd_mid", [3, NE * C], BF16)
        bd_low, bd_some = sb("bd_low", [3, NE * C], BF16), sb("bd_some", [3, NE * C], BF16)
        bd3 = sb("bd3", [3, NE * C], BF16)
        ident = sb("ident", [P, P])
        ones_row = sb("ones_row", [1, P])
        before = sb("before", [P, P], BF16)
        ones_bf = sb("ones_bf", [P, P], BF16)
        far = sb("far", [P, P], BF16)
        half = sb("half", [P, TPG])
        first = sb("first", [P, NE])
        carry_i = sb("carry_i", [P, NE], I32)
        carry = sb("carry", [P, NE])
        region0 = sb("region0", [P, NE])
        upto = sb("upto", [P, NE, NE])
        tile_i = sb("tile_i", [P, NT], I32)
        tile_no = sb("tile_no", [P, NT])
        padrow = sb("padrow", [P, ROW])
        tok_i = sb("tok_i", [P, TPG], I32)
        tok = sb("tok", [P, TPG])
        first_i = sb("first_i", [P, NE], I32)

        spare = sb("spare", [1, 256])
        turn = sb("turn", [1, RING])
        used_spare = [0]

        xb = sb("xb", [P, RING, TPG, C])
        adjb = sb("adjb", [P, 2, TPG, P], I32)
        maskb = sb("maskb", [P, 2, TPG, P], BF16)
        bn = sb("bn", [P, 2, TPG, 6])
        mv = sb("mv", [P, 2, TPG, 2])
        ve = sb("ve", [P, 2, TPG])
        rstd = sb("rstd", [P, 2, TPG])
        fn = sb("fn", [P, 2, TPG, C])
        fT = sb("fT", [P, RING, N])
        gT = sb("gT", [P, 2, N])
        f2 = sb("f2", [P, RING, TPG, C])
        vcol = sb("vcol", [P, 2, TPG])
        lg = sb("lg", [P, 2, TPG, P])
        relu = sb("relu", [P, 2, TPG, P])
        nmax = sb("nmax", [P, 2, TPG])
        pr = sb("pr", [P, 2, TPG, P])
        psumr = sb("psumr", [P, 2, TPG])
        rsum = sb("rsum", [P, 2, TPG])
        pT = sb("pT", [P, 2, N])
        ex = sb("ex", [P, 2, TPG, C])
        rr = sb("rr", [P, 2, TPG, C])
        rowb = sb("rowb", [P, RING, TPG, ROW])
        bn2 = sb("bn2", [P, 2, TPG, 6])
        ve2 = sb("ve2", [P, 2, TPG])
        xn2 = sb("xn2", [P, 2, TPG, C])
        xT_hi, xT_lo = sb("xT_hi", [P, 2, N], F32R), sb("xT_lo", [P, 2, N], F32R)
        hT = sb("hT", [P, 2, NCH, N])
        gS = sb("gS", [P, 2, N])
        gsum = sb("gsum", [P, 2, TPG, NE])
        gl = sb("gl", [P, 2, TPG, NE])
        gmx = sb("gmx", [P, 2, TPG])
        gd = sb("gd", [P, 2, TPG, NE])
        ge = sb("ge", [P, 2, TPG, NE])
        gs = sb("gs", [P, 2, TPG])
        hit = sb("hit", [P, 2, TPG, NE])
        hmx = sb("hmx", [P, 2, TPG])
        hot = sb("hot", [P, 2, TPG, NE], BF16)
        pos = sb("pos", [P, 2, TPG, NE])
        pos2 = sb("pos2", [P, 2, TPG, NE])
        dest = sb("dest", [P, 2, TPG])
        desti = sb("desti", [P, RING, TPG], I32)

        cnt = sb("cnt", [P, NE])
        cnti = sb("cnti", [P, NE], I32)
        cntj = sb("cntj", [P, NE], I32)
        ntile = sb("ntile", [P, NE])
        upn = sb("upn", [P, NE, NE])
        incl = sb("incl", [P, NE])
        gain = sb("gain", [P, NE])
        past = sb("past", [1, NT, NE])
        past2 = sb("past2", [1, NT, NE])
        tex = sb("tex", [1, NT])
        tst = sb("tst", [1, NT])
        trow = sb("trow", [1, NT])
        row_tab = sb("row_tab", [1, NT], I32)
        wd_tab = sb("wd_tab", [1, NT], I32)
        next_row = sb("next_row", [P, NE], I32)

        crow = rowb
        cxn, chT = xn2, hT
        cx_hi, cx_lo = xT_hi, xT_lo
        cout = xb
        ctok = desti

        ps = ctx.enter_context(nc.psum_tensor("ps", [P, 8, 512], F32))
        B_TR, B_G, B_L, B_F2, B_SM, B_H, B_HID = 0, 1, 2, 3, 4, 5, 6
        HID_BANK = (B_HID, B_HID + 1, B_F2, B_HID)
        B_Y = 2
        F2_IN = 3
        ps_f2 = ps[:, B_F2, 0:F2_IN * (C + 1)].rearrange("p (t c) -> p t c", t=F2_IN)
        ps_f2b = ps[:, B_SM, 256:256 + C + 1].rearrange("p (t c) -> p t c", t=1)
        ps_gate = ps[:, B_TR, :].rearrange("p (t h e) -> p t e h", t=TPG, e=QUAD)[:, :, 0:NE, :]
        ps_rank = ps[:, B_SM, 128:128 + TPG * NE].rearrange("p (t e) -> p t e", e=NE)
        ps_tot = ps[:, B_SM, 192:192 + NE]

        def bank(b):
            return ps[:, b, :].rearrange("p (t c) -> p t c", t=TPG)

        gat_loaded, w_loaded, bd_loaded, wd_loaded = (
            sem(n) for n in ("gat_loaded", "w_loaded", "bd_loaded", "wd_loaded"))
        w1_parts, bd_parts = sem("w1_parts"), sem("bd_parts")
        ident_ok = sem("ident_ok")
        consts = sem("consts")
        setup_pe, setup_dve = sem("setup_pe"), sem("setup_dve")
        x_in = [sem(f"x_in{i}") for i in range(RING)]
        adj_in = [sem(f"adj_in{i}") for i in range(2)]
        names = ["stats", "var_eps", "rstd_ok", "fn_ok", "fT_ps", "fT_ok", "g_ps", "gT_ok", "f2_ps", "f2_ok", "vcol_ok",
                 "lg_ps", "relu_ok", "mask_ok", "leaky_ok", "nmax_ok", "probs", "rsum_ok", "probs_n", "pT_ps", "pT_ok",
                 "hout_ps", "expm", "elu_neg", "elu_pos", "x2_ok", "bn_ok", "bn2_ok",
                 "stats2", "var_eps2", "rstd2_ok", "xn_ok", "xT_ps", "xT_ok", "xlo_ok", "hid_ps", "hid_ok",
                 "gcol_ps", "gS_ok", "gate_ps", "gsum_ok", "gl_ok", "gmx_ok", "gd_ok", "gate_exp", "gs_ok",
                 "prob_ok", "hit0", "hit1", "hmx_ok", "hot_ok",
                 "rank_ps", "pos_ok", "tok_ok", "tok_next", "carried", "pos_hot", "dest_ok", "desti_ok"]
        S = {n: sem(n) for n in names}
        sent = [sem(f"sent{i}") for i in range(2)]
        pads_sent = sem("pads_sent")
        pad0_sent = sem("pad0_sent")
        tab = sem("tab")
        pads_ready = sem("pads_ready")
        row_tab_ok, wd_tab_ok = sem("row_tab_ok"), sem("wd_tab_ok")
        rows_in = [sem(f"rows_in{i}") for i in range(RING)]
        out_sent = [sem(f"out_sent{i}") for i in range(2)]
        C_ = {n: sem("c_" + n) for n in ["xn", "xT_ps", "x_hi", "x_lo", "hid_ps", "hid", "y_ps", "out", "turn", "ids"]}

        def hold(eng, *waits):
            waits = [w for w in waits if w]
            for s, n in waits:
                eng.wait_ge(s, n)
            if any(not isinstance(n, int) for _, n in waits):
                one = spare[:, used_spare[0]:used_spare[0] + 1]
                used_spare[0] += 1
                if eng.engine == mybir.EngineType.Pool:
                    nc.gpsimd.tensor_tensor(one, half[0:1, 0:1], half[0:1, 0:1], ALU.add)
                else:
                    nc.vector.memset(one, 0.0)

        def plain(eng, wait):
            if wait:
                eng.wait_ge(*wait)

        def of(sem_, g, ago=0, per=1):
            n = (g.n - ago + 1) * per
            return None if isinstance(n, int) and n <= 0 else (sem_, n)

        def landed(sem_, g, per, ago=0):
            if isinstance(g.n, int):
                n = ((g.n - g.two) // 2 + 1 - ago // 2) * 16 * per
                return (sem_, n) if n > 0 else None
            return (sem_, (g.n + (2 - g.two - ago)) * (8 * per))

        block = ctx.enter_context(nc.Block())
        x_g = x.rearrange("(g t) n c -> g n t c", t=TPG)
        adj_g = adj.rearrange("(g t) n m -> g n t m", t=TPG)
        out_rows = out.rearrange("b n c -> (b n) c")

        def pad(eng, experts):
            eng.wait_ge(pads_ready, 1)
            for e in experts:
                r = eng.value_load(next_row[0:1, e:e + 1], min_val=0, max_val=NE * REGION - P)
                eng.dma_start(rows[bass.ds(r, P), :], padrow[:]).then_inc(pads_sent, 16)

        def scratch_full(eng):
            for s in sent:
                eng.wait_ge(s, 16 * TPG * NG // 2)
            eng.wait_ge(pads_sent, 16 * NE)
            eng.wait_ge(pad0_sent, 16)
            eng.wait_ge(row_tab_ok, 1)

        @block.sync
        def _(sp):
            def load_weights(n):
                if n == 0:
                    for dst, src in ((w_sb[:], g_w), (a12_sb[:], g_a12), (a_sb[:, 0:1], g_a1), (a_sb[:, 1:2], g_a2),
                                     (w2v[:, 0:C], g_w2), (bg[0:1, :], f_bg.rearrange("(o e) -> o e", o=1))):
                        sp.dma_start(dst, src, allow_slow_non_contiguous=True).then_inc(gat_loaded, 16)
                if n == 1:
                    sp.wait_ge(consts, 21)
                    for dst, src in ((w1g[:], g_w1), (w1f[:], f_w1), (b1f[:], f_b1.rearrange("(h p) -> p h", p=P)),
                                     (wg[:, :, 0:NE], f_wg.rearrange("(h p) e -> p h e", p=P))):
                        sp.dma_start(dst, src, allow_slow_non_contiguous=True).then_inc(w_loaded, 16)
                if n == 3:
                    for k in range(3):
                        sp.dma_start(bd[k:k + 1, :], f_bd.rearrange("(o e) c -> o (e c)", o=1)).then_inc(bd_loaded, 16)
                    sp.dma_start(wd[:].rearrange("p (e h c) -> p e h c", e=NE, h=NCH),
                                 f_wd.rearrange("e (h p) c -> p e h c", p=P)).then_inc(wd_loaded, 16)

            def load(t):
                g = back(t, 0, NG)
                if g is None:
                    return
                after(sp, S["elu_pos"], g, RING)
                if not isinstance(g.n, int):
                    sp.dma_start(xb[:, g.ring], x_g[bass.ds(g.n, 1)].rearrange("o n t c -> (o n) t c")
                                 ).then_inc(x_in[g.ring], 16)
                elif g.n != 3:
                    sp.dma_start(xb[:, g.ring], x_g[g.n]).then_inc(x_in[g.ring], 16)
                if isinstance(g.n, int) and g.n == 0:
                    load_weights(0)
                if isinstance(g.n, int) and g.n == 2:
                    sp.dma_start(xb[:, 3], x_g[3]).then_inc(x_in[3], 16)
                after(sp, S["mask_ok"], g, 2)
                sp.dma_start(adjb[:, g.two], adj_g[g.n] if isinstance(g.n, int) else
                             adj_g[bass.ds(g.n, 1)].rearrange("o n t c -> (o n) t c")).then_inc(adj_in[g.two], 16)
                if isinstance(g.n, int) and g.n > 0:
                    load_weights(g.n)

            slots(sp, load, NG, 0, PEEL1)

            pad(sp, range(0, NE, 2))
            scratch_full(sp)

            def load_rows(t):
                q = back(t, 0, NQ)
                if q is None:
                    return
                after(sp, C_["out"], q, RING)
                for b in range(TPG // 2 if isinstance(q.n, int) and q.n < 2 else TPG):
                    r = sp.value_load(row_tab[0:1, bass.ds(q.n * TPG + b, 1)], min_val=0, max_val=NE * REGION)
                    sp.dma_start(crow[:, q.ring, b, :], rows[bass.ds(r, P), :]).then_inc(rows_in[q.ring], 16)

            slots(sp, load_rows, NQ, 0, PEEL2)
            for i in range(2):
                sp.wait_ge(out_sent[i], 16 * TPG * NQ // 2)

        @block.gpsimd
        def _(pool):
            nc.gpsimd.memset(ident[:], 0.0).then_inc(ident_ok, 1)
            pool.wait_ge(ident_ok, 1)
            nc.gpsimd.affine_select(out=ident[:], in_=ident[:], compare_op=ALU.not_equal, fill=1.0, base=0,
                                    pattern=[[-1, P]], channel_multiplier=1).then_inc(ident_ok, 1)
            nc.gpsimd.memset(before[:], 0.0).then_inc(consts, 1)
            nc.gpsimd.memset(ones_bf[:], 1.0).then_inc(consts, 1)
            nc.gpsimd.memset(far[:], 0.0).then_inc(consts, 1)
            nc.gpsimd.memset(ones_row[:], 1.0).then_inc(consts, 1)
            nc.gpsimd.memset(half[:], -0.5).then_inc(consts, 1)
            nc.gpsimd.memset(upto[:], 1.0).then_inc(consts, 1)
            nc.gpsimd.memset(padrow[:], 0.0).then_inc(consts, 1)
            nc.gpsimd.iota(first_i[:], pattern=[[-1, NE]], base=NE, channel_multiplier=0).then_inc(consts, 1)
            nc.gpsimd.iota(carry_i[:], pattern=[[REGION, NE]], base=0, channel_multiplier=0).then_inc(consts, 1)
            nc.gpsimd.iota(tile_i[:], pattern=[[1, NT]], base=0, channel_multiplier=0).then_inc(consts, 1)
            nc.gpsimd.iota(tok_i[:], pattern=[[P, TPG]], base=0, channel_multiplier=1).then_inc(consts, 1)
            nc.gpsimd.memset(wg[:], 0.0).then_inc(consts, 1)
            pool.wait_ge(consts, 12)
            nc.gpsimd.affine_select(out=far[:], in_=far[:], compare_op=ALU.not_equal, fill=NEG / SLOPE, base=0,
                                    pattern=[[-1, P]], channel_multiplier=1).then_inc(consts, 1)
            nc.gpsimd.affine_select(out=before[:], in_=before[:], compare_op=ALU.is_ge, fill=1.0, base=0,
                                    pattern=[[-1, P]], channel_multiplier=1).then_inc(consts, 1)
            nc.gpsimd.affine_select(out=upto[:], in_=upto[:], compare_op=ALU.is_ge, fill=0.0, base=0,
                                    pattern=[[1, NE], [-1, NE]], channel_multiplier=0).then_inc(consts, 1)
            nc.gpsimd.iota(padrow[:, TOKEN:TOKEN + 1].bitcast(I32), pattern=[[0, 1]], base=TOKENS,
                           channel_multiplier=0).then_inc(consts, 1)
            nc.gpsimd.tensor_copy(first[:], first_i[:]).then_inc(consts, 1)
            nc.gpsimd.tensor_copy(carry[:], carry_i[:]).then_inc(consts, 1)
            nc.gpsimd.tensor_copy(region0[:], carry_i[:]).then_inc(consts, 1)
            nc.gpsimd.tensor_copy(tile_no[:], tile_i[:]).then_inc(consts, 1)
            nc.gpsimd.tensor_copy(tok[:], tok_i[:]).then_inc(consts, 1)
            pool.wait_ge(consts, 21)
            pool.dma_start(rows[NE * REGION:NE * REGION + P, :], padrow[:]).then_inc(pad0_sent, 16)

            def power(t, by, stats, var_eps, ve_, var_of, out_of, done, used):
                g = back(t, by, NG)
                if g is None:
                    return
                hold(pool, of(S[stats], g))
                nc.gpsimd.tensor_scalar(ve_[:, g.two], var_of(g), EPS, None, ALU.add).then_inc(S[var_eps], 1)
                hold(pool, of(S[var_eps], g), of(S[used], g, 2))
                nc.gpsimd.tensor_tensor(out_of(g), ve_[:, g.two], half[:], ALU.pow).then_inc(S[done], 1)

            def add(t):
                g = back(t, 4, NG)
                if g is None:
                    return
                after(pool, S["elu_pos"], g)
                after(pool, S["elu_neg"], g)
                plain(pool, landed(sent[g.two], g, TPG, RING))
                nc.gpsimd.tensor_tensor(rowb[:, g.ring, :, 0:C], ex[:, g.two], rr[:, g.two],
                                        ALU.add).then_inc(S["x2_ok"], 1)

            def number(t):
                g = back(t, 6, NG)
                if g is None:
                    return
                hold(pool, of(S["x2_ok"], g), of(S["tok_next"], g, 1))
                nc.gpsimd.tensor_copy(rowb[:, g.ring, :, TOKEN].bitcast(I32), tok[:]).then_inc(S["tok_ok"], 1)
                hold(pool, of(S["tok_ok"], g))
                nc.gpsimd.tensor_scalar(tok[:], tok[:], float(N), None, ALU.add).then_inc(S["tok_next"], 1)

            def send(t, tiles):
                g = back(t, 7, NG)
                if g is None:
                    return
                if tiles[0] == 0:
                    hold(pool, of(S["desti_ok"], g), of(S["prob_ok"], g), of(S["rstd2_ok"], g),
                         of(S["tok_ok"], g), landed(sent[g.two], g, TPG, 2))
                for b in tiles:
                    nc.gpsimd.indirect_dma_start(
                        rows[:, :], bass.IndirectOffsetOnAxis(desti[:, g.ring, b:b + 1], 0),
                        rowb[:, g.ring, b, :], None,
                        bounds_check=NE * REGION - 1, oob_is_err=False).then_inc(sent[g.two], 16)

            def slot(t):
                add(t)
                send(t, range(TPG))
                power(t, 4, "stats2", "var_eps2", ve2, lambda g: rowb[:, g.ring, :, RSTD],
                      lambda g: rowb[:, g.ring, :, RSTD], "rstd2_ok", "xn_ok")
                power(t, 0, "stats", "var_eps", ve, lambda g: mv[:, g.two, :, 1],
                      lambda g: rstd[:, g.two], "rstd_ok", "fn_ok")
                number(t)

            slots(pool, slot, NG, DEPTH1, PEEL1)

            def send_out(t):
                q = back(t, 4, NQ)
                if q is None:
                    return
                plain(pool, of(C_["out"], q))
                plain(pool, of(C_["ids"], q))
                plain(pool, landed(out_sent[q.two], q, TPG, 2))
                nc.gpsimd.tensor_tensor(turn[:, q.ring:q.ring + 1], half[0:1, 0:1], half[0:1, 0:1],
                                        ALU.add).then_inc(C_["turn"], 1)
                for b in range(TPG):
                    nc.gpsimd.indirect_dma_start(
                        out_rows[:, :],
                        bass.IndirectOffsetOnAxis(ctok[:, q.ring, b:b + 1], 0),
                        cout[:, q.ring, b, :], None,
                        bounds_check=TOKENS - 1, oob_is_err=False).then_inc(out_sent[q.two], 16)

            slots(pool, send_out, NQ, DEPTH2, PEEL2)

        @block.tensor
        def _(pe):
            pe.wait_ge(ident_ok, 2)
            pe.wait_ge(gat_loaded, 16 * 6)
            nc.tensor.transpose(ps[:, 0, 0:P], w_sb[:], ident[:])
            nc.tensor.transpose(ps[:, 0, P:2 * P], a12_sb[:], ident[:]).then_inc(setup_pe, 1)
            pe.wait_ge(consts, 21)
            pe.wait_ge(setup_dve, 2)
            nc.tensor.matmul(ps[:, 1, 0:C], a12T[:], wT[:], start=True, stop=True)
            nc.tensor.matmul(ps[:, 1, 256:258], wT[:], a_sb[:], start=True, stop=True)
            nc.tensor.matmul(ps[:, 1, 320:320 + NE], ones_row[:], bg[0:1, :], start=True,
                             stop=True).then_inc(setup_pe, 1)
            pe.wait_ge(setup_dve, 6)
            nc.tensor.matmul(ps[:, 2, 0:C], wT[:], a12wT[:], start=True, stop=True).then_inc(setup_pe, 1)
            pe.wait_ge(setup_dve, 7)

            def t_fT(t):
                g = back(t, 1, NG)
                if g is None:
                    return
                after(pe, S["fn_ok"], g)
                after(pe, S["elu_pos"], g, 3)
                after(pe, S["expm"], g, 3)
                for b in range(TPG):
                    m = nc.tensor.transpose(bank(B_H)[:, b, :], fn[:, g.two, b, :], ident[:])
                m.then_inc(S["fT_ps"], 1)

            def t_g(t):
                g = back(t, 1, NG)
                if g is None:
                    return
                after(pe, S["fT_ok"], g)
                after(pe, S["gT_ok"], g, 1)
                after(pe, S["pT_ok"], g, 2)
                nc.tensor.matmul(ps[:, B_G, :], pair[:], fT[:, g.ring], start=True, stop=True).then_inc(S["g_ps"], 1)

            def t_f2(t):
                g = back(t, 2, NG)
                if g is None:
                    return
                after(pe, S["f2_ok"], g, 1)
                n = (g.n - 4) * NCH + 3
                if not (isinstance(n, int) and n <= 0):
                    pe.wait_ge(S["hid_ok"], n)
                after(pe, S["pos_ok"], g, 5)
                after(pe, S["carried"], g, 5)
                for b in range(TPG):
                    m = nc.tensor.matmul(ps_f2[:, b, :] if b < F2_IN else ps_f2b[:, 0, :],
                                         fT[:, g.ring, b * P:(b + 1) * P], w2v[:], start=True, stop=True)
                m.then_inc(S["f2_ps"], 1)

            def t_lg(t):
                g = back(t, 2, NG)
                if g is None:
                    return
                after(pe, S["gT_ok"], g)
                after(pe, S["fT_ok"], g)
                after(pe, S["mask_ok"], g)
                after(pe, S["leaky_ok"], g, 1)
                for b in range(TPG):
                    nc.tensor.matmul(bank(B_L)[:, b, :], far[:], maskb[:, g.two, b, :], start=True, stop=False)
                    m = nc.tensor.matmul(bank(B_L)[:, b, :], gT[:, g.two, b * P:(b + 1) * P],
                                         fT[:, g.ring, b * P:(b + 1) * P], start=False, stop=True)
                m.then_inc(S["lg_ps"], 1)

            def t_pT(t):
                g = back(t, 3, NG)
                if g is None:
                    return
                after(pe, S["probs_n"], g)
                after(pe, S["gS_ok"], g, 3)
                for b in range(TPG):
                    m = nc.tensor.transpose(bank(B_G)[:, b, :], pr[:, g.two, b, :], ident[:])
                m.then_inc(S["pT_ps"], 1)

            def t_hout(t):
                g = back(t, 3, NG)
                if g is None:
                    return
                if isinstance(g.n, int) and g.n == 0:
                    pe.wait_ge(w_loaded, 16 * 4)
                after(pe, S["pT_ok"], g)
                after(pe, S["f2_ok"], g)
                after(pe, S["elu_pos"], g, 1)
                after(pe, S["expm"], g, 1)
                after(pe, S["fT_ok"], g, -2, last=NG)
                for b in range(TPG):
                    nc.tensor.matmul(bank(B_H)[:, b, :], fT[:, g.ring, b * P:(b + 1) * P], w1g[:], start=True,
                                     stop=False)
                    m = nc.tensor.matmul(bank(B_H)[:, b, :], pT[:, g.two, b * P:(b + 1) * P], f2[:, g.ring, b, :],
                                         start=False, stop=True)
                m.then_inc(S["hout_ps"], 1)

            def t_xT(t):
                g = back(t, 5, NG)
                if g is None:
                    return
                after(pe, S["xn_ok"], g)
                after(pe, S["xT_ok"], g, 1)
                after(pe, S["xlo_ok"], g, 1)
                after(pe, S["gsum_ok"], g, 2)
                for b in range(TPG):
                    m = nc.tensor.transpose(bank(B_TR)[:, b, :], xn2[:, g.two, b, :], ident[:])
                m.then_inc(S["xT_ps"], 1)

            def hidden(h, acc, hi, lo):
                w_hi, w_lo = w1_hi[:, h * P:(h + 1) * P], w1_lo[:, h * P:(h + 1) * P]
                nc.tensor.matmul(acc, w_hi, hi, start=True, stop=False)
                nc.tensor.matmul(acc, w_lo, hi, start=False, stop=False)
                return nc.tensor.matmul(acc, w_hi, lo, start=False, stop=True)

            def t_hid(t, chunks):
                g = back(t, 5, NG)
                if g is None:
                    return
                if isinstance(g.n, int) and g.n == 0:
                    pe.wait_ge(w1_parts, 2)
                after(pe, S["xT_ok"], g)
                after(pe, S["xlo_ok"], g)
                for h in chunks:
                    n = g.n * NCH + (0, -2, -2, 1)[h]
                    if not (isinstance(n, int) and n <= 0):
                        pe.wait_ge(S["hid_ok"], n)
                    if h == 2:
                        after(pe, S["f2_ok"], g, -3, last=NG)
                    hidden(h, ps[:, HID_BANK[h], :], xT_hi[:, g.two], xT_lo[:, g.two]).then_inc(S["hid_ps"], 1)

            def t_gcol(t):
                g = back(t, 6, NG)
                if g is None:
                    return
                after(pe, S["hid_ok"], g, 0, NCH)
                after(pe, S["gT_ok"], g, -4, last=NG)
                after(pe, S["gS_ok"], g, 1)
                for h in range(NCH):
                    m = nc.tensor.matmul(ps[QUAD * h:QUAD * (h + 1), B_G, :], wg[:, h, :], hT[:, g.two, h, :],
                                         start=True, stop=True)
                m.then_inc(S["gcol_ps"], 1)

            def t_gate(t):
                g = back(t, 6, NG)
                if g is None:
                    return
                after(pe, S["gS_ok"], g)
                after(pe, S["xT_ok"], g, -1, last=NG)
                after(pe, S["xlo_ok"], g, -1, last=NG)
                for b in range(TPG):
                    m = nc.tensor.transpose(bank(B_TR)[:, b, :], gS[:, g.two, b * P:(b + 1) * P], ident[:])
                m.then_inc(S["gate_ps"], 1)

            def t_rank(t):
                g = back(t, 6, NG)
                if g is None:
                    return
                after(pe, S["hot_ok"], g)
                after(pe, S["pos_ok"], g, 1)
                after(pe, S["carried"], g, 1)
                after(pe, S["f2_ok"], g, -4, last=NG)
                for b in range(TPG):
                    nc.tensor.matmul(ps_rank[:, b, :], before[:], hot[:, g.two, b, :], start=True, stop=(b == 0))
                    for a in range(b):
                        nc.tensor.matmul(ps_rank[:, b, :], ones_bf[:], hot[:, g.two, a, :], start=False,
                                         stop=(a == b - 1))
                for b in range(TPG):
                    m = nc.tensor.matmul(ps_tot, ones_bf[:], hot[:, g.two, b, :], start=(b == 0), stop=(b == TPG - 1))
                m.then_inc(S["rank_ps"], 1)

            def slot(t):
                t_gcol(t)
                t_xT(t)
                t_f2(t)
                t_lg(t)
                t_fT(t)
                t_pT(t)
                t_hid(t, (0,))
                t_hid(t, (1,))
                t_g(t)
                t_gate(t)
                t_hid(t, (2, 3))
                t_hout(t)
                t_rank(t)

            slots(pe, slot, NG, DEPTH1, PEEL1)

            pe.wait_ge(wd_tab_ok, 1)
            pe.wait_ge(wd_loaded, 16)

            def c_xT(t):
                q = back(t, 1, NQ)
                if q is None:
                    return
                after(pe, C_["xn"], q)
                after(pe, C_["x_lo"], q, 1)
                for b in range(TPG):
                    m = nc.tensor.transpose(bank(B_TR)[:, b, :], cxn[:, q.two, b, :], ident[:])
                m.then_inc(C_["xT_ps"], 1)

            def c_hid(t, h):
                q = back(t, 2, NQ)
                if q is None:
                    return
                after(pe, C_["x_hi"], q)
                after(pe, C_["x_lo"], q)
                n = q.n * NCH + h - 1
                if not (isinstance(n, int) and n <= 0):
                    pe.wait_ge(C_["hid"], n)
                hidden(h, ps[:, B_HID + h % 2, :], cx_hi[:, q.two], cx_lo[:, q.two]).then_inc(C_["hid_ps"], 1)

            def c_experts(t):
                q = back(t, 3, NQ)
                if q is None:
                    return
                return nc.values_load_multi_w_load_instructions(
                    wd_tab[0:1, bass.ds(q.n * TPG, TPG)], [mybir.EngineType.PE], min_val=0, max_val=NE - 1)[1]

            def c_y(t, experts, b):
                q = back(t, 3, NQ)
                if q is None:
                    return
                w = experts[b]
                if isinstance(q.n, int) and q.n == 0:
                    pe.wait_ge(bd_parts, 7)
                after(pe, C_["hid"], q, 0, NCH)
                after(pe, C_["out"], q, 2)
                nc.tensor.matmul(bank(B_Y + q.two)[:, b, :], ones_bf[0:3, :], bd3[:, bass.ds(w * C, C)],
                                 start=True, stop=False)
                for h in range(NCH):
                    m = nc.tensor.matmul(bank(B_Y + q.two)[:, b, :], chT[:, q.two, h, b * P:(b + 1) * P],
                                         wd[:, bass.ds(w * (NCH * C) + h * C, C)], start=False,
                                         stop=(h == NCH - 1))
                m.then_inc(C_["y_ps"], 1)

            def slot_c(t):
                experts = c_experts(t)
                c_hid(t, 0)
                c_y(t, experts, 0)
                c_hid(t, 1)
                c_y(t, experts, 1)
                c_xT(t)
                c_hid(t, 2)
                c_y(t, experts, 2)
                c_hid(t, 3)
                c_y(t, experts, 3)

            slots(pe, slot_c, NQ, DEPTH2, PEEL2)

        @block.scalar
        def _(act):
            act.wait_ge(setup_dve, 7)

            def a_fT(t):
                g = back(t, 1, NG)
                if g is None:
                    return
                after(act, S["fT_ps"], g)
                after(act, S["hout_ps"], g, RING)
                nc.scalar.copy(fT[:, g.ring], ps[:, B_H, :]).then_inc(S["fT_ok"], 1)

            def a_gT(t):
                g = back(t, 1, NG)
                if g is None:
                    return
                after(act, S["g_ps"], g)
                after(act, S["lg_ps"], g, 2)
                nc.scalar.activation(gT[:, g.two], ps[:, B_G, :], ACT.Identity, bias=uv[:, 0:1]).then_inc(S["gT_ok"], 1)

            def a_pT(t):
                g = back(t, 3, NG)
                if g is None:
                    return
                after(act, S["pT_ps"], g)
                after(act, S["hout_ps"], g, 2)
                nc.scalar.copy(pT[:, g.two], ps[:, B_G, :]).then_inc(S["pT_ok"], 1)

            def a_gS(t):
                g = back(t, 6, NG)
                if g is None:
                    return
                after(act, S["gcol_ps"], g)
                after(act, S["gate_ps"], g, 2)
                nc.scalar.copy(gS[:, g.two], ps[:, B_G, :]).then_inc(S["gS_ok"], 1)

            def a_relu(t):
                g = back(t, 2, NG)
                if g is None:
                    return
                after(act, S["lg_ps"], g)
                after(act, S["vcol_ok"], g)
                after(act, S["leaky_ok"], g, 2)
                for b in range(TPG):
                    m = nc.scalar.activation(relu[:, g.two, b, :], bank(B_L)[:, b, :], ACT.Relu,
                                             bias=vcol[:, g.two, b:b + 1], scale=1.0 - SLOPE)
                m.then_inc(S["relu_ok"], 1)

            def a_exp(t):
                g = back(t, 3, NG)
                if g is None:
                    return
                after(act, S["nmax_ok"], g)
                after(act, S["pT_ps"], g, 2)
                after(act, S["rsum_ok"], g, 2)
                for b in range(TPG):
                    nc.scalar.activation(pr[:, g.two, b, :], lg[:, g.two, b, :], ACT.Exp, bias=nmax[:, g.two, b:b + 1],
                                         accum_out=psumr[:, g.two, b:b + 1]).then_inc(S["probs"], 1)

            def a_expm(t):
                g = back(t, 4, NG)
                if g is None:
                    return
                after(act, S["hout_ps"], g)
                after(act, S["x2_ok"], g, 2)
                nc.scalar.activation(ex[:, g.two], bank(B_H), ACT.Exp).then_inc(S["expm"], 1)

            def a_xT(t):
                g = back(t, 5, NG)
                if g is None:
                    return
                after(act, S["xT_ps"], g)
                after(act, S["hid_ps"], g, 2, NCH)
                nc.scalar.copy(xT_hi[:, g.two], ps[:, B_TR, :]).then_inc(S["xT_ok"], 1)

            def a_gelu(t, chunks):
                g = back(t, 5, NG)
                if g is None:
                    return
                after(act, S["gcol_ps"], g, 2)
                for h in chunks:
                    act.wait_ge(S["hid_ps"], g.n * NCH + (h + 1))
                    nc.scalar.activation(hT[:, g.two, h, :], ps[:, HID_BANK[h], :], ACT.Gelu,
                                         bias=b1f[:, h:h + 1]).then_inc(S["hid_ok"], 1)

            def a_gate(t):
                g = back(t, 7, NG)
                if g is None:
                    return
                after(act, S["gd_ok"], g)
                after(act, S["gs_ok"], g, 2)
                nc.scalar.activation(ge[:, g.two], gd[:, g.two], ACT.Exp).then_inc(S["gate_exp"], 1)

            def slot(t):
                a_gate(t)
                a_expm(t)
                a_exp(t)
                a_xT(t)
                a_gS(t)
                a_relu(t)
                a_fT(t)
                a_pT(t)
                a_gelu(t, (0, 1))
                a_gT(t)
                a_gelu(t, (2, 3))

            slots(act, slot, NG, DEPTH1, PEEL1)

            pad(act, range(1, NE, 2))
            scratch_full(act)
            for q in range(2):
                for b in range(TPG // 2, TPG):
                    r = act.value_load(row_tab[0:1, q * TPG + b:q * TPG + b + 1], min_val=0, max_val=NE * REGION)
                    act.dma_start(crow[:, q, b, :], rows[bass.ds(r, P), :]).then_inc(rows_in[q], 16)

            def c_hi(t):
                q = back(t, 1, NQ)
                if q is None:
                    return
                after(act, C_["xT_ps"], q)
                after(act, C_["x_lo"], q, 2)
                after(act, C_["hid_ps"], q, 2, NCH)
                nc.scalar.copy(cx_hi[:, q.two], ps[:, B_TR, :]).then_inc(C_["x_hi"], 1)

            def c_gelu(t, chunks):
                q = back(t, 2, NQ)
                if q is None:
                    return
                after(act, C_["y_ps"], q, 2, TPG)
                for h in chunks:
                    act.wait_ge(C_["hid_ps"], q.n * NCH + (h + 1))
                    nc.scalar.activation(chT[:, q.two, h, :], ps[:, B_HID + h % 2, :], ACT.Gelu,
                                         bias=b1f[:, h:h + 1]).then_inc(C_["hid"], 1)

            def slot_c(t):
                c_gelu(t, (0, 1))
                c_hi(t)
                c_gelu(t, (2, 3))

            slots(act, slot_c, NQ, DEPTH2, PEEL2)

        @block.vector
        def _(dve):
            V = nc.vector
            def weights():
                dve.wait_ge(setup_pe, 1)
                V.tensor_copy(wT[:], ps[:, 0, 0:P]).then_inc(setup_dve, 1)
                V.tensor_copy(a12T[:], ps[:, 0, P:2 * P]).then_inc(setup_dve, 1)
                dve.wait_ge(setup_pe, 2)
                V.tensor_copy(a12wT[:], ps[:, 1, 0:C]).then_inc(setup_dve, 1)
                V.tensor_copy(uv[:], ps[:, 1, 256:258]).then_inc(setup_dve, 1)
                V.tensor_copy(w2v[:, C:C + 1], ps[:, 1, 257:258]).then_inc(setup_dve, 1)
                V.tensor_copy(bg[:], ps[:, 1, 320:320 + NE]).then_inc(setup_dve, 1)
                dve.wait_ge(setup_pe, 3)
                V.tensor_copy(pair[:], ps[:, 2, 0:C]).then_inc(setup_dve, 1)
                dve.wait_ge(setup_dve, 7)

            def split_w1():
                dve.wait_ge(w_loaded, 16 * 4)
                V.tensor_copy(w1_hi[:], w1f[:]).then_inc(w1_parts, 1)
                dve.wait_ge(w1_parts, 1)
                V.tensor_tensor(w1_lo[:], w1f[:], w1_hi[:].bitcast(F32), ALU.subtract).then_inc(w1_parts, 1)

            def split_bias_high():
                dve.wait_ge(ident_ok, 2)
                dve.wait_ge(bd_loaded, 16 * 3)
                V.tensor_copy(bd_hi[:], bd[:]).then_inc(bd_parts, 1)
                dve.wait_ge(bd_parts, 1)
                V.tensor_tensor(bd_rest[:], bd[:], bd_hi[:], ALU.subtract).then_inc(bd_parts, 1)
                V.tensor_scalar(bd_some[:], bd_hi[:], ident[0:3, 0:1], None, ALU.mult).then_inc(bd_parts, 1)
                dve.wait_ge(bd_parts, 2)
                V.tensor_copy(bd_mid[:], bd_rest[:]).then_inc(bd_parts, 1)

            def split_bias_low():
                dve.wait_ge(bd_parts, 4)
                V.tensor_tensor(bd_low[:], bd_rest[:], bd_mid[:], ALU.subtract).then_inc(bd_parts, 1)
                V.scalar_tensor_tensor(bd_some[:], bd_mid[:], ident[0:3, 1:2], bd_some[:], ALU.mult,
                                       ALU.add).then_inc(bd_parts, 1)

            def split_bias_last():
                dve.wait_ge(bd_parts, 6)
                V.scalar_tensor_tensor(bd3[:], bd_low[:], ident[0:3, 2:3], bd_some[:], ALU.mult,
                                       ALU.add).then_inc(bd_parts, 1)

            def x_ready(g):
                if isinstance(g.n, int):
                    dve.wait_ge(x_in[g.ring], 16 * (g.n // RING + 1))
                else:
                    dve.wait_ge(x_in[g.ring], (g.n + (RING - g.ring)) * (16 // RING))

            def d_stats(t):
                g = back(t, 0, NG)
                if g is None:
                    return
                x_ready(g)
                after(dve, S["var_eps"], g, 2)
                for b in range(TPG):
                    m = V.bn_stats(bn[:, g.two, b, :], xb[:, g.ring, b, :])
                m.then_inc(S["bn_ok"], 1)

            def d_aggr(t):
                g = back(t, 0, NG)
                if g is None:
                    return
                hold(dve, of(S["bn_ok"], g))
                for b in range(TPG):
                    m = V.bn_aggr(mv[:, g.two, b, :], bn[:, g.two, b, :])
                m.then_inc(S["stats"], 1)

            def d_norm(t):
                g = back(t, 1, NG)
                if g is None:
                    return
                after(dve, S["rstd_ok"], g)
                after(dve, S["fT_ps"], g, 2)
                for b in range(TPG):
                    m = V.tensor_scalar(fn[:, g.two, b, :], xb[:, g.ring, b, :], mv[:, g.two, b, 0:1],
                                        rstd[:, g.two, b:b + 1], ALU.subtract, ALU.mult)
                m.then_inc(S["fn_ok"], 1)

            def d_v(t):
                g = back(t, 2, NG)
                if g is None:
                    return
                after(dve, S["f2_ps"], g)
                after(dve, S["relu_ok"], g, 2)
                V.tensor_scalar(vcol[:, g.two, 0:F2_IN], ps_f2[:, :, C], 1.0 - SLOPE, None, ALU.mult)
                V.tensor_scalar(vcol[:, g.two, F2_IN:TPG], ps_f2b[:, :, C], 1.0 - SLOPE, None,
                                ALU.mult).then_inc(S["vcol_ok"], 1)

            def d_f2(t):
                g = back(t, 2, NG)
                if g is None:
                    return
                after(dve, S["f2_ps"], g)
                after(dve, S["hout_ps"], g, RING)
                V.tensor_copy(f2[:, g.ring, 0:F2_IN], ps_f2[:, :, 0:C])
                V.tensor_copy(f2[:, g.ring, F2_IN:TPG], ps_f2b[:, :, 0:C]).then_inc(S["f2_ok"], 1)

            def d_leaky(t):
                g = back(t, 2, NG)
                if g is None:
                    return
                after(dve, S["relu_ok"], g)
                after(dve, S["probs"], g, 2, TPG)
                V.scalar_tensor_tensor(lg[:, g.two], bank(B_L), SLOPE, relu[:, g.two], ALU.mult,
                                       ALU.add).then_inc(S["leaky_ok"], 1)

            def d_mask(t):
                g = back(t, 1, NG)
                if g is None:
                    return
                plain(dve, landed(adj_in[g.two], g, 1))
                after(dve, S["lg_ps"], g, 2)
                V.tensor_scalar(maskb[:, g.two], adjb[:, g.two], 0, None, ALU.is_le).then_inc(S["mask_ok"], 1)

            def d_max(t):
                g = back(t, 2, NG)
                if g is None:
                    return
                after(dve, S["leaky_ok"], g)
                after(dve, S["probs"], g, 2, TPG)
                V.tensor_reduce(nmax[:, g.two], lg[:, g.two], AX.X, ALU.max, negate=True).then_inc(S["nmax_ok"], 1)

            def d_probs(t):
                g = back(t, 3, NG)
                if g is None:
                    return
                after(dve, S["probs"], g, 0, TPG)
                V.reciprocal(rsum[:, g.two], psumr[:, g.two]).then_inc(S["rsum_ok"], 1)

            def d_probs_n(t):
                g = back(t, 3, NG)
                if g is None:
                    return
                after(dve, S["rsum_ok"], g)
                V.tensor_tensor(pr[:, g.two], pr[:, g.two], rsum[:, g.two].unsqueeze(2).to_broadcast([P, TPG, P]),
                                ALU.mult).then_inc(S["probs_n"], 1)

            def d_elu(t):
                g = back(t, 4, NG)
                if g is None:
                    return
                after(dve, S["hout_ps"], g)
                after(dve, S["x2_ok"], g, 2)
                after(dve, S["expm"], g)
                V.scalar_tensor_tensor(rr[:, g.two], bank(B_H), 0.0, xb[:, g.ring], ALU.max,
                                       ALU.add).then_inc(S["elu_pos"], 1)
                V.tensor_scalar(ex[:, g.two], ex[:, g.two], 1.0, -1.0, ALU.min, ALU.add).then_inc(S["elu_neg"], 1)

            def d_stats2(t):
                g = back(t, 4, NG)
                if g is None:
                    return
                after(dve, S["x2_ok"], g)
                for b in range(TPG):
                    m = V.bn_stats(bn2[:, g.two, b, :], rowb[:, g.ring, b, 0:C])
                m.then_inc(S["bn2_ok"], 1)

            def d_aggr2(t):
                g = back(t, 4, NG)
                if g is None:
                    return
                hold(dve, of(S["bn2_ok"], g), of(S["var_eps2"], g, 2))
                for b in range(TPG):
                    m = V.bn_aggr(rowb[:, g.ring, b, MEAN:MEAN + 2], bn2[:, g.two, b, :])
                m.then_inc(S["stats2"], 1)

            def d_norm2(t):
                g = back(t, 5, NG)
                if g is None:
                    return
                after(dve, S["rstd2_ok"], g)
                after(dve, S["xT_ps"], g, 2)
                for b in range(TPG):
                    m = V.tensor_scalar(xn2[:, g.two, b, :], rowb[:, g.ring, b, 0:C], rowb[:, g.ring, b, MEAN:MEAN + 1],
                                        rowb[:, g.ring, b, RSTD:RSTD + 1], ALU.subtract, ALU.mult)
                m.then_inc(S["xn_ok"], 1)

            def d_xlo(t):
                g = back(t, 5, NG)
                if g is None:
                    return
                after(dve, S["xT_ok"], g)
                after(dve, S["hid_ps"], g, 2, NCH)
                V.tensor_tensor(xT_lo[:, g.two], ps[:, B_TR, :], xT_hi[:, g.two].bitcast(F32),
                                ALU.subtract).then_inc(S["xlo_ok"], 1)

            def wide(v):
                return v.unsqueeze(2).to_broadcast([P, TPG, NE])

            def d_gate(t, k):
                g = back(t, 6, NG)
                if g is None:
                    return
                if k == 0:
                    after(dve, S["gate_ps"], g)
                    V.tensor_reduce(gsum[:, g.two], ps_gate, AX.X, ALU.add).then_inc(S["gsum_ok"], 1)
                if k == 1:
                    after(dve, S["gsum_ok"], g)
                    V.tensor_tensor(gl[:, g.two], gsum[:, g.two], bg[:].unsqueeze(1).to_broadcast([P, TPG, NE]),
                                    ALU.add).then_inc(S["gl_ok"], 1)
                if k == 2:
                    after(dve, S["gl_ok"], g)
                    V.tensor_reduce(gmx[:, g.two], gl[:, g.two], AX.X, ALU.max).then_inc(S["gmx_ok"], 1)
                if k == 3:
                    after(dve, S["gmx_ok"], g)
                    after(dve, S["gate_exp"], g, 2)
                    V.tensor_tensor(gd[:, g.two], gl[:, g.two], wide(gmx[:, g.two]),
                                    ALU.subtract).then_inc(S["gd_ok"], 1)
                    V.tensor_tensor(hit[:, g.two], gl[:, g.two], wide(gmx[:, g.two]),
                                    ALU.is_equal).then_inc(S["hit0"], 1)
                if k == 4:
                    after(dve, S["hit0"], g)
                    V.tensor_tensor(hit[:, g.two], hit[:, g.two], first[:].unsqueeze(1).to_broadcast([P, TPG, NE]),
                                    ALU.mult).then_inc(S["hit1"], 1)
                if k == 5:
                    after(dve, S["hit1"], g)
                    V.tensor_reduce(hmx[:, g.two], hit[:, g.two], AX.X, ALU.max).then_inc(S["hmx_ok"], 1)
                if k == 6:
                    after(dve, S["hmx_ok"], g)
                    after(dve, S["rank_ps"], g, 2)
                    V.tensor_tensor(hot[:, g.two], hit[:, g.two], wide(hmx[:, g.two]),
                                    ALU.is_equal).then_inc(S["hot_ok"], 1)

            def d_prob(t, k):
                g = back(t, 7, NG)
                if g is None:
                    return
                if k == 0:
                    after(dve, S["gate_exp"], g)
                    V.tensor_reduce(gs[:, g.two], ge[:, g.two], AX.X, ALU.add).then_inc(S["gs_ok"], 1)
                if k == 1:
                    after(dve, S["gs_ok"], g)
                    V.reciprocal(rowb[:, g.ring, :, PROB], gs[:, g.two]).then_inc(S["prob_ok"], 1)

            def d_route(t, k):
                g = back(t, 7, NG)
                if g is None:
                    return
                if k == 0:
                    after(dve, S["rank_ps"], g)
                    after(dve, S["carried"], g, 1)
                    V.tensor_tensor(pos[:, g.two], ps_rank, carry[:].unsqueeze(1).to_broadcast([P, TPG, NE]),
                                    ALU.add).then_inc(S["pos_ok"], 1)
                if k == 1:
                    after(dve, S["pos_ok"], g)
                    V.tensor_tensor(carry[:], ps_tot, carry[:], ALU.add).then_inc(S["carried"], 1)
                    V.tensor_tensor(pos2[:, g.two], pos[:, g.two], hot[:, g.two], ALU.mult).then_inc(S["pos_hot"], 1)
                if k == 2:
                    after(dve, S["pos_hot"], g)
                    V.tensor_reduce(dest[:, g.two], pos2[:, g.two], AX.X, ALU.add).then_inc(S["dest_ok"], 1)
                if k == 3:
                    after(dve, S["dest_ok"], g)
                    V.tensor_copy(desti[:, g.ring], dest[:, g.two]).then_inc(S["desti_ok"], 1)

            def slot(t):
                filling = isinstance(t.n, int) and t.n < RING
                if filling:
                    d_stats(t)
                    d_aggr(t)
                    if t.n == 0:
                        weights()
                    if t.n == 2:
                        split_w1()
                d_norm2(t)
                d_route(t, 0)
                d_prob(t, 0)
                d_route(t, 1)
                d_norm(t)
                d_route(t, 2)
                d_prob(t, 1)
                d_elu(t)
                d_route(t, 3)
                d_probs(t)
                d_v(t)
                d_probs_n(t)
                d_xlo(t)
                draining = isinstance(t.n, int) and t.n >= NG + 4
                if draining:
                    (split_bias_high, split_bias_last, lambda: None)[t.n - NG - 4]()
                d_f2(t)
                d_stats2(t)
                d_leaky(t)
                d_aggr2(t)
                if not filling:
                    d_stats(t)
                d_gate(t, 0)
                if not filling:
                    d_aggr(t)
                d_gate(t, 1)
                d_max(t)
                d_gate(t, 2)
                d_mask(t)
                d_gate(t, 3)
                d_gate(t, 4)
                d_gate(t, 5)
                d_gate(t, 6)
                if draining and t.n == NG + 4:
                    split_bias_low()

            slots(dve, slot, NG, DEPTH1, PEEL1)

            done = [0]

            def step(ins):
                done[0] += 1
                ins.then_inc(tab, 1)
                dve.wait_ge(tab, done[0])

            dve.wait_ge(S["carried"], NG)
            V.tensor_copy(next_row[:], carry[:]).then_inc(pads_ready, 1)
            step(V.tensor_tensor(cnt[:], carry[:], region0[:], ALU.subtract))
            step(V.tensor_scalar(cnti[:], cnt[:], float(P - 1), None, ALU.add))
            step(V.tensor_scalar(cntj[:], cnti[:], 7, None, ALU.arith_shift_right))
            step(V.tensor_copy(ntile[:], cntj[:]))
            step(V.tensor_tensor(upn[:], upto[:], ntile[:].unsqueeze(1).to_broadcast([P, NE, NE]), ALU.mult))
            step(V.tensor_reduce(incl[:], upn[:], AX.X, ALU.add))
            step(V.tensor_scalar(gain[:], ntile[:], -float(P), float(REGION), ALU.mult, ALU.add))
            step(V.tensor_tensor(past[:], tile_no[0:1].unsqueeze(2).to_broadcast([1, NT, NE]),
                                 incl[0:1].unsqueeze(1).to_broadcast([1, NT, NE]), ALU.is_ge))
            step(V.tensor_tensor(past2[:], past[:], gain[0:1].unsqueeze(1).to_broadcast([1, NT, NE]), ALU.mult))
            step(V.tensor_reduce(tst[:], past2[:], AX.X, ALU.add))
            step(V.scalar_tensor_tensor(trow[:], tile_no[0:1], float(P), tst[:], ALU.mult, ALU.add))
            V.tensor_scalar(row_tab[:], trow[:], float(NE * REGION), None, ALU.min).then_inc(row_tab_ok, 1)
            step(V.tensor_reduce(tex[:], past[:], AX.X, ALU.add))
            V.tensor_scalar(wd_tab[:], tex[:], float(NE - 1), None, ALU.min).then_inc(wd_tab_ok, 1)

            def c_norm(t):
                q = back(t, 1, NQ)
                if q is None:
                    return
                if isinstance(q.n, int):
                    dve.wait_ge(rows_in[q.ring], 16 * TPG * (q.n // RING + 1))
                else:
                    dve.wait_ge(rows_in[q.ring], (q.n + (RING - q.ring)) * (16 * TPG // RING))
                after(dve, C_["xT_ps"], q, 2)
                for b in range(TPG):
                    m = V.tensor_scalar(cxn[:, q.two, b, :], crow[:, q.ring, b, 0:C], crow[:, q.ring, b, MEAN:MEAN + 1],
                                        crow[:, q.ring, b, RSTD:RSTD + 1], ALU.subtract, ALU.mult)
                m.then_inc(C_["xn"], 1)

            def c_lo(t):
                q = back(t, 1, NQ)
                if q is None:
                    return
                after(dve, C_["xT_ps"], q)
                after(dve, C_["x_hi"], q)
                after(dve, C_["hid_ps"], q, 2, NCH)
                V.tensor_tensor(cx_lo[:, q.two], ps[:, B_TR, :], cx_hi[:, q.two].bitcast(F32),
                                ALU.subtract).then_inc(C_["x_lo"], 1)

            def c_out(t):
                q = back(t, 3, NQ)
                if q is None:
                    return
                plain(dve, landed(out_sent[q.two], q, TPG, RING))
                plain(dve, of(C_["turn"], q, RING))
                V.tensor_copy(ctok[:, q.ring], crow[:, q.ring, :, TOKEN].bitcast(I32)).then_inc(C_["ids"], 1)
                after(dve, C_["y_ps"], q, 0, TPG)
                for b in range(TPG):
                    m = V.scalar_tensor_tensor(cout[:, q.ring, b, :], bank(B_Y + q.two)[:, b, :],
                                               crow[:, q.ring, b, PROB:PROB + 1], crow[:, q.ring, b, 0:C],
                                               ALU.mult, ALU.add)
                m.then_inc(C_["out"], 1)

            def slot_c(t):
                c_norm(t)
                c_lo(t)
                c_out(t)

            slots(dve, slot_c, NQ, DEPTH2, PEEL2)


INPUTS = ["x", "adj", "L0_gnn_W", "L0_gnn_a_1", "L0_gnn_a_2", "L0_gnn_a_12", "L0_gnn_W_1", "L0_gnn_W_2",
          "L0_ffn_W1", "L0_ffn_b1", "L0_ffn_Wg", "L0_ffn_bg", "L0_ffn_Wd", "L0_ffn_bd"]


def kernel(**inputs):
    import numpy as np
    import concourse.bacc as bacc
    from concourse.bass_utils import run_bass_kernel_spmd

    nc = bacc.Bacc("TRN2", target_bir_lowering=False, num_devices=1)
    arrays, args = {}, []
    for name in INPUTS:
        a = np.ascontiguousarray(inputs[name])
        arrays[name] = a
        args.append(nc.dram_tensor(name, a.shape, mybir.dt.from_np(a.dtype), kind="ExternalInput").ap())
    nb, n, _ = inputs["x"].shape
    ne = inputs["L0_ffn_Wd"].shape[0]
    rows = nc.dram_tensor("rows", (ne * (nb * n + P) + P, ROW), F32).ap()
    out = nc.dram_tensor("out", inputs["x"].shape, F32, kind="ExternalOutput").ap()
    build(nc, *args, rows, out)
    return run_bass_kernel_spmd(nc, [arrays], core_ids=[0]).results[0]["out"]
```
